# Optimizing a Trainium2 kernel written in Bass

```python
import numpy as np
import jax
import jax.numpy as jnp

def _softmax(x, axis=-1):
    return jax.nn.softmax(x, axis=axis)

def _gelu(x):
    return jax.nn.gelu(x, approximate=True)

def _silu(x):
    return jax.nn.silu(x)

def _sigmoid(x):
    return jax.nn.sigmoid(x)

def _layernorm(x, axis=-1, eps=1e-05):
    m = jnp.mean(x, axis=axis, keepdims=True)
    v = jnp.var(x, axis=axis, keepdims=True)
    return (x - m) / jnp.sqrt(v + eps)

def _scatter_add(tgt, idx, src, axis=0):
    return tgt.at[idx].add(src)

def _segment_sum(src, seg, n):
    return jax.ops.segment_sum(src, seg, n)
kernel_name = 'mk_flamingo_gated_d2_seqx_r4_b9a48d'

def setup_inputs(seed: int=0):
    np.random.seed(seed)
    _w = jnp.asarray

    def _rec_inputs():
        import jax
        import jax.numpy as jnp
        _rk = jax.random.key(seed)
        x = -0.0002928 + 1 * jax.random.normal(jax.random.fold_in(_rk, 1), (16, 112, 256), jnp.float32)
        _lenS = 112 - jax.random.randint(jax.random.fold_in(_rk, 7), (16,), 0, max(1, 112 // 4) + 1, jnp.int32)
        _lenS2 = 375 - jax.random.randint(jax.random.fold_in(_rk, 8), (16,), 0, max(1, 375 // 4) + 1, jnp.int32)
        _ctx_1024P = jax.random.normal(jax.random.fold_in(_rk, 11), (16, 16, 256), jnp.float32)
        _ctx_1024c = jax.random.dirichlet(jax.random.fold_in(_rk, 511), 0.3 * jnp.ones((16,), jnp.float32), (16, 375))
        _ctx_1024t = jnp.einsum('bsk,bkd->bsd', _ctx_1024c, _ctx_1024P)
        _ctx_1024t = _ctx_1024t * jax.lax.rsqrt(jnp.mean(jnp.square(_ctx_1024t)) + 1e-12) * 0.953939
        ctx_1024 = -1.39393e-06 + 0.999914 * (_ctx_1024t + 0.3 * jax.random.normal(jax.random.fold_in(_rk, 611), (16, 375, 256), jnp.float32))
        _g = jax.random.normal(jax.random.fold_in(_rk, 9001), (2, 2), jnp.float32)
        _g = jnp.sign(_g) * jnp.maximum(jnp.abs(_g), 1.0) + (_g == 0) * 1.0
        g_xattn = _g[0]
        g_ffn = _g[1]
        return (x, ctx_1024, g_xattn, g_ffn)
    x, ctx_1024, g_xattn, g_ffn = _rec_inputs()

    def _L0_xattn_setup():
        import jax, jax.numpy as jnp
        import numpy as np
        HIDDEN = 256
        NUM_HEADS = 16
        HEAD_DIM = HIDDEN // NUM_HEADS
        key = jax.random.key(seed)
        ks = jax.random.split(key, 10)
        B, T, S = (2, 512, 512)
        sc = 1.0 / np.sqrt(HIDDEN)
        inp = {'tgt': jax.random.normal(ks[0], (B, T, HIDDEN), jnp.float32), 'src': jax.random.normal(ks[1], (B, S, HIDDEN), jnp.float32), 'Wq': jax.random.normal(ks[2], (NUM_HEADS, HIDDEN, HEAD_DIM), jnp.float32) * sc, 'bq': jnp.zeros((NUM_HEADS, HEAD_DIM), jnp.float32), 'Wk': jax.random.normal(ks[3], (NUM_HEADS, HIDDEN, HEAD_DIM), jnp.float32) * sc, 'bk': jnp.zeros((NUM_HEADS, HEAD_DIM), jnp.float32), 'Wv': jax.random.normal(ks[4], (NUM_HEADS, HIDDEN, HEAD_DIM), jnp.float32) * sc, 'bv': jnp.zeros((NUM_HEADS, HEAD_DIM), jnp.float32), 'Wo': jax.random.normal(ks[5], (HIDDEN, HIDDEN), jnp.float32) * sc, 'bo': jnp.zeros((HIDDEN,), jnp.float32)}
        return inp
    _L0_xattn_all = _L0_xattn_setup()
    _L0_xattn_in = {k: v for k, v in _L0_xattn_all.items() if k in ('Wq', 'bq', 'Wk', 'bk', 'Wv', 'bv', 'Wo', 'bo')}
    del _L0_xattn_all

    def _L0_ffn_setup():
        import jax, jax.numpy as jnp
        import numpy as np
        D_MODEL = 256
        HIDDEN = 512
        E_ROUTED = 14
        E_SHARED = 2
        TOP_K = 2
        EPS = 1e-09
        RMS_EPS = 1.1920929e-07

        def _ffn(xn, rw, W1, W2):
            ms = jnp.mean(xn * xn, axis=-1, keepdims=True)
            h = xn * jax.lax.rsqrt(ms + RMS_EPS) * rw
            return jax.nn.silu(h @ W1) @ W2
        key = jax.random.key(seed)
        ks = jax.random.split(key, 9)
        B, T = (2, 256)
        x = jax.random.normal(ks[0], (B, T, D_MODEL), dtype=jnp.float32)
        router_w = jax.random.normal(ks[1], (D_MODEL, E_ROUTED), dtype=jnp.float32) * 0.006
        rms_w = jnp.ones((E_ROUTED, D_MODEL), dtype=jnp.float32)
        w1 = jax.random.normal(ks[2], (E_ROUTED, D_MODEL, HIDDEN), dtype=jnp.float32) * 0.02
        w2 = jax.random.normal(ks[3], (E_ROUTED, HIDDEN, D_MODEL), dtype=jnp.float32) * 0.02
        rms_w_s = jnp.ones((E_SHARED, D_MODEL), dtype=jnp.float32)
        w1_s = jax.random.normal(ks[4], (E_SHARED, D_MODEL, HIDDEN), dtype=jnp.float32) * 0.02
        w2_s = jax.random.normal(ks[5], (E_SHARED, HIDDEN, D_MODEL), dtype=jnp.float32) * 0.02
        return {'x': x, 'router_w': router_w, 'rms_w': rms_w, 'w1': w1, 'w2': w2, 'rms_w_s': rms_w_s, 'w1_s': w1_s, 'w2_s': w2_s}
    _L0_ffn_all = _L0_ffn_setup()
    _L0_ffn_in = {k: v for k, v in _L0_ffn_all.items() if k in ('router_w', 'rms_w', 'w1', 'w2', 'rms_w_s', 'w1_s', 'w2_s')}
    del _L0_ffn_all

    def _L1_xattn_setup():
        import jax, jax.numpy as jnp
        import numpy as np
        C = 256
        B, SQ, SKV = (4, 512, 512)
        key = jax.random.key(seed)
        ks = jax.random.split(key, 10)
        s = 1.0 / np.sqrt(C)
        return {'x': jax.random.normal(ks[0], (B, SQ, C), jnp.float32), 'content_embeddings': jax.random.normal(ks[1], (B, SKV, C), jnp.float32), 'Wq': jax.random.normal(ks[2], (C, C), jnp.float32) * s, 'bq': jnp.zeros((C,), jnp.float32), 'Wk': jax.random.normal(ks[3], (C, C), jnp.float32) * s, 'bk': jnp.zeros((C,), jnp.float32), 'Wv': jax.random.normal(ks[4], (C, C), jnp.float32) * s, 'bv': jnp.zeros((C,), jnp.float32), 'Wo': jax.random.normal(ks[5], (C, C), jnp.float32) * s, 'bo': jnp.zeros((C,), jnp.float32)}
    _L1_xattn_all = _L1_xattn_setup()
    _L1_xattn_in = {k: v for k, v in _L1_xattn_all.items() if k in ('Wq', 'bq', 'Wk', 'bk', 'Wv', 'bv', 'Wo', 'bo')}
    del _L1_xattn_all

    def _L1_ffn_setup():
        import jax, jax.numpy as jnp
        import numpy as np
        EPS_LN = 1e-05
        EPS_GATE = 1e-08

        def layer_norm(x, gamma, beta):
            mu = jnp.mean(x, axis=-1, keepdims=True)
            var = jnp.mean(jnp.square(x - mu), axis=-1, keepdims=True)
            return (x - mu) * jax.lax.rsqrt(var + EPS_LN) * gamma + beta
        key = jax.random.key(seed)
        ks = jax.random.split(key, 8)
        B, S, D, E, H = (4, 1024, 256, 4, 512)
        s_in = 1.0 / np.sqrt(D)
        s_h = 1.0 / np.sqrt(H)
        return {'h': jax.random.normal(ks[0], (B, S, D), dtype=jnp.float32), 'router_w': jax.random.uniform(ks[1], (E, D), jnp.float32, -s_in, s_in), 'rn_g': jnp.ones((D,), jnp.float32), 'rn_b': jnp.zeros((D,), jnp.float32), 'w1': jax.random.uniform(ks[2], (E, D, H), jnp.float32, -s_in, s_in), 'ln_g': jnp.ones((E, H), jnp.float32), 'ln_b': jnp.zeros((E, H), jnp.float32), 'w2': jax.random.uniform(ks[3], (E, H, D), jnp.float32, -s_h, s_h), 'on_g': jnp.ones((D,), jnp.float32), 'on_b': jnp.zeros((D,), jnp.float32)}
    _L1_ffn_all = _L1_ffn_setup()
    _L1_ffn_in = {k: v for k, v in _L1_ffn_all.items() if k in ('router_w', 'rn_g', 'rn_b', 'w1', 'ln_g', 'ln_b', 'w2', 'on_g', 'on_b')}
    del _L1_ffn_all
    return {'x': x, 'ctx_1024': ctx_1024, 'g_xattn': g_xattn, 'g_ffn': g_ffn, 'L0_xattn_Wq': _L0_xattn_in['Wq'], 'L0_xattn_bq': _L0_xattn_in['bq'], 'L0_xattn_Wk': _L0_xattn_in['Wk'], 'L0_xattn_bk': _L0_xattn_in['bk'], 'L0_xattn_Wv': _L0_xattn_in['Wv'], 'L0_xattn_bv': _L0_xattn_in['bv'], 'L0_xattn_Wo': _L0_xattn_in['Wo'], 'L0_xattn_bo': _L0_xattn_in['bo'], 'L0_ffn_router_w': _L0_ffn_in['router_w'], 'L0_ffn_rms_w': _L0_ffn_in['rms_w'], 'L0_ffn_w1': _L0_ffn_in['w1'], 'L0_ffn_w2': _L0_ffn_in['w2'], 'L0_ffn_rms_w_s': _L0_ffn_in['rms_w_s'], 'L0_ffn_w1_s': _L0_ffn_in['w1_s'], 'L0_ffn_w2_s': _L0_ffn_in['w2_s'], 'L1_xattn_Wq': _L1_xattn_in['Wq'], 'L1_xattn_bq': _L1_xattn_in['bq'], 'L1_xattn_Wk': _L1_xattn_in['Wk'], 'L1_xattn_bk': _L1_xattn_in['bk'], 'L1_xattn_Wv': _L1_xattn_in['Wv'], 'L1_xattn_bv': _L1_xattn_in['bv'], 'L1_xattn_Wo': _L1_xattn_in['Wo'], 'L1_xattn_bo': _L1_xattn_in['bo'], 'L1_ffn_router_w': _L1_ffn_in['router_w'], 'L1_ffn_rn_g': _L1_ffn_in['rn_g'], 'L1_ffn_rn_b': _L1_ffn_in['rn_b'], 'L1_ffn_w1': _L1_ffn_in['w1'], 'L1_ffn_ln_g': _L1_ffn_in['ln_g'], 'L1_ffn_ln_b': _L1_ffn_in['ln_b'], 'L1_ffn_w2': _L1_ffn_in['w2'], 'L1_ffn_on_g': _L1_ffn_in['on_g'], 'L1_ffn_on_b': _L1_ffn_in['on_b']}

def reference(x, ctx_1024, g_xattn, g_ffn, L0_xattn_Wq, L0_xattn_bq, L0_xattn_Wk, L0_xattn_bk, L0_xattn_Wv, L0_xattn_bv, L0_xattn_Wo, L0_xattn_bo, L0_ffn_router_w, L0_ffn_rms_w, L0_ffn_w1, L0_ffn_w2, L0_ffn_rms_w_s, L0_ffn_w1_s, L0_ffn_w2_s, L1_xattn_Wq, L1_xattn_bq, L1_xattn_Wk, L1_xattn_bk, L1_xattn_Wv, L1_xattn_bv, L1_xattn_Wo, L1_xattn_bo, L1_ffn_router_w, L1_ffn_rn_g, L1_ffn_rn_b, L1_ffn_w1, L1_ffn_ln_g, L1_ffn_ln_b, L1_ffn_w2, L1_ffn_on_g, L1_ffn_on_b):
    import jax
    import jax.numpy as jnp

    def _L0_xattn_ref(tgt, src, Wq, bq, Wk, bk, Wv, bv, Wo, bo):
        import jax, jax.numpy as jnp
        import numpy as np
        HIDDEN = 256
        NUM_HEADS = 16
        HEAD_DIM = HIDDEN // NUM_HEADS
        q = jnp.einsum('btd,hdk->bhtk', tgt, Wq) + bq[None, :, None, :]
        k = jnp.einsum('bsd,hdk->bhsk', src, Wk) + bk[None, :, None, :]
        v = jnp.einsum('bsd,hdk->bhsk', src, Wv) + bv[None, :, None, :]
        scale = 1.0 / jnp.sqrt(jnp.asarray(HEAD_DIM, q.dtype))
        scores = jnp.einsum('bhtk,bhsk->bhts', q, k) * scale
        weights = jax.nn.softmax(scores, axis=-1)
        out = jnp.einsum('bhts,bhsk->bhtk', weights, v)
        B, H, T, Dh = out.shape
        h = out.transpose(0, 2, 1, 3).reshape(B, T, H * Dh)
        return h @ Wo + bo

    def _L0_ffn_ref(x, router_w, rms_w, w1, w2, rms_w_s, w1_s, w2_s):
        import jax, jax.numpy as jnp
        import numpy as np
        D_MODEL = 256
        HIDDEN = 512
        E_ROUTED = 14
        E_SHARED = 2
        TOP_K = 2
        EPS = 1e-09
        RMS_EPS = 1.1920929e-07

        def _ffn(xn, rw, W1, W2):
            ms = jnp.mean(xn * xn, axis=-1, keepdims=True)
            h = xn * jax.lax.rsqrt(ms + RMS_EPS) * rw
            return jax.nn.silu(h @ W1) @ W2
        B, T, D = x.shape
        N = B * T
        xf = x.reshape(N, D)
        gates = jax.nn.softmax(xf @ router_w, axis=-1)
        top_v, top_i = jax.lax.top_k(gates, TOP_K)
        masked = jnp.zeros_like(gates).at[jnp.arange(N)[:, None], top_i].set(top_v)
        masked = masked / (masked.sum(axis=-1, keepdims=True) + EPS)
        routed = jax.vmap(lambda rw_, W1_, W2_: _ffn(xf, rw_, W1_, W2_))(rms_w, w1, w2)
        routed_out = jnp.einsum('end,ne->nd', routed, masked)
        shared = jax.vmap(lambda rw_, W1_, W2_: _ffn(xf, rw_, W1_, W2_))(rms_w_s, w1_s, w2_s).sum(0)
        return (routed_out + shared).reshape(B, T, D)

    def _L1_xattn_ref(x, content_embeddings, Wq, bq, Wk, bk, Wv, bv, Wo, bo):
        import jax, jax.numpy as jnp
        import numpy as np
        C = 256
        B, SQ, SKV = (4, 512, 512)
        queries = x @ Wq.T + bq
        keys = content_embeddings @ Wk.T + bk
        values = content_embeddings @ Wv.T + bv
        scale = 1.0 / jnp.sqrt(jnp.asarray(C, x.dtype))
        scores = jnp.einsum('bqc,bkc->bqk', queries, keys) * scale
        attn = jax.nn.softmax(scores, axis=-1)
        attended = jnp.einsum('bqk,bkc->bqc', attn, values)
        out = x + attended
        return out @ Wo.T + bo

    def _L1_ffn_ref(h, router_w, rn_g, rn_b, w1, ln_g, ln_b, w2, on_g, on_b):
        import jax, jax.numpy as jnp
        import numpy as np
        EPS_LN = 1e-05
        EPS_GATE = 1e-08

        def layer_norm(x, gamma, beta):
            mu = jnp.mean(x, axis=-1, keepdims=True)
            var = jnp.mean(jnp.square(x - mu), axis=-1, keepdims=True)
            return (x - mu) * jax.lax.rsqrt(var + EPS_LN) * gamma + beta
        D = h.shape[-1]
        h_norm = layer_norm(h, rn_g, rn_b)
        g = jax.nn.softmax(jnp.einsum('bsd,ed->bse', h_norm, router_w), axis=-1)
        top2_w, top2_idx = jax.lax.top_k(g, 2)
        top2_w = top2_w / (jnp.sum(top2_w, axis=-1, keepdims=True) + EPS_GATE)
        hid = jnp.einsum('bsd,edh->bseh', h, w1)
        hid = jax.nn.relu(layer_norm(hid, ln_g, ln_b))
        expert_out = jnp.einsum('bseh,ehd->bsed', hid, w2)
        idx = jnp.broadcast_to(top2_idx[..., None], top2_idx.shape + (D,))
        top2_out = jnp.take_along_axis(expert_out, idx, axis=-2)
        out = jnp.sum(top2_out * top2_w[..., None], axis=-2)
        return layer_norm(out, on_g, on_b)
    x = x + jnp.tanh(g_xattn[0]) * _L0_xattn_ref(_layernorm(x, axis=-1), ctx_1024, L0_xattn_Wq, L0_xattn_bq, L0_xattn_Wk, L0_xattn_bk, L0_xattn_Wv, L0_xattn_bv, L0_xattn_Wo, L0_xattn_bo)
    x = x + jnp.tanh(g_ffn[0]) * _L0_ffn_ref(_layernorm(x, axis=-1), L0_ffn_router_w, L0_ffn_rms_w, L0_ffn_w1, L0_ffn_w2, L0_ffn_rms_w_s, L0_ffn_w1_s, L0_ffn_w2_s)
    x = x + jnp.tanh(g_xattn[1]) * _L1_xattn_ref(_layernorm(x, axis=-1), ctx_1024, L1_xattn_Wq, L1_xattn_bq, L1_xattn_Wk, L1_xattn_bk, L1_xattn_Wv, L1_xattn_bv, L1_xattn_Wo, L1_xattn_bo)
    x = x + jnp.tanh(g_ffn[1]) * _L1_ffn_ref(_layernorm(x, axis=-1), L1_ffn_router_w, L1_ffn_rn_g, L1_ffn_rn_b, L1_ffn_w1, L1_ffn_ln_g, L1_ffn_ln_b, L1_ffn_w2, L1_ffn_on_g, L1_ffn_on_b)
    return x

_drawn_inputs = setup_inputs


def setup_inputs(seed=0):
    import zlib

    import numpy as np

    out = dict(_drawn_inputs(seed))
    spreads = {'g_ffn': (-1.0, 0.2),
     'L0_xattn_bq': (0.0, 0.1),
     'L0_xattn_bk': (0.0, 0.1),
     'L0_xattn_bv': (0.0, 0.1),
     'L0_xattn_bo': (0.0, 0.1),
     'L0_ffn_rms_w': (1.0, 0.2),
     'L0_ffn_rms_w_s': (1.0, 0.2),
     'L1_xattn_bq': (0.0, 0.1),
     'L1_xattn_bk': (0.0, 0.1),
     'L1_xattn_bv': (0.0, 0.1),
     'L1_xattn_bo': (0.0, 0.1),
     'L1_ffn_rn_g': (1.0, 0.2),
     'L1_ffn_rn_b': (0.0, 0.1),
     'L1_ffn_ln_g': (1.0, 0.2),
     'L1_ffn_ln_b': (0.0, 0.1),
     'L1_ffn_on_g': (1.0, 0.2),
     'L1_ffn_on_b': (0.0, 0.1)}
    factors = {}
    for name, (base, spread) in spreads.items():
        noise = np.random.default_rng([zlib.crc32(name.encode()), seed]).standard_normal(out[name].shape)
        drawn = base * np.exp(spread * noise) if base else spread * noise
        out[name] = jnp.asarray(drawn.astype(out[name].dtype))
    for name, factor in factors.items():
        out[name] = (out[name] * factor).astype(out[name].dtype)
    return out
```

```python
from contextlib import ExitStack

import concourse.bass as bass
from concourse import mybir

ALU = mybir.AluOpType
ACT = mybir.ActivationFunctionType
AX = mybir.AxisListType.X
F32 = mybir.dt.float32
BF16 = mybir.dt.bfloat16
U32 = mybir.dt.uint32

P = 128
B, T, D = 16, 112, 256
S, SC, C = 375, 3, 125
KD = D // P
H, DH = 16, 16
N = B * T
GB = 4
NG = B // GB
GT = GB * T
HID = 512
HM = HID // P
E0, E0S, E1 = 14, 2, 4
QW = 2 * T
LN_EPS = 1e-5
RMS_EPS = 1.1920929e-07
L0_GATE_EPS, L1_GATE_EPS = 1e-9, 1e-8


def at_least(engine, sem, value):
    if isinstance(value, int) and value <= 0:
        return
    engine.wait_ge(sem, value)


def three_products(nc, out, left, right, first=True, last=True):
    steps = []
    for (lh, ll), (rh, rl) in zip(left, right):
        steps += [(lh, rh), (ll, rh), (lh, rl)]
    for i, (l, r) in enumerate(steps):
        ins = nc.tensor.matmul(out, l, r, start=first and i == 0, stop=last and i == len(steps) - 1)
    return ins


class Core:

    def __init__(self, nc, ctx):
        self.nc, self.ctx = nc, ctx
        self.sems = []
        self.xs = self.sb("xs", [T, B, D], F32)
        self.xn = self.sb("xn", [T, B, D], F32)
        self.xT = [self.sb(f"xT_{p}", [P, KD, N], BF16) for p in ("hi", "lo")]
        self.ident = self.sb("ident", [P, P], F32)
        self.g_x = self.sb("g_x", [P, 2], F32)
        self.g_f = self.sb("g_f", [P, 2], F32)
        self.tg_x = self.sb("tg_x", [P, 2], F32)
        self.tg_f = self.sb("tg_f", [P, 2], F32)
        self.mv = self.sb("mv", [T, B, 2], F32)
        self.rstd = self.sb("rstd", [T, B], F32)
        self.ps = ctx.enter_context(nc.psum_tensor("ps", [P, 8, 512], F32))

    def sb(self, name, shape, dt, ctx=None):
        return (ctx or self.ctx).enter_context(self.nc.sbuf_tensor(name, shape, dt))

    def sem(self, name):
        self.sems.append(self.nc.alloc_semaphore(name=name))
        return self.sems[-1]

    def release(self):
        self.nc.all_engine_barrier()
        self.nc.clear_and_free_semaphores(self.sems)
        self.nc.all_engine_barrier()
        self.sems = []


def setup(nc, k, x, g_xattn, g_ffn):
    x_in, g_in, id_zero, id_done, tanh_done = (k.sem("setup_" + s) for s in
                                               ("x_in", "g_in", "id_zero", "id_done", "tanh"))
    with nc.Block() as block:
        @block.sync
        def _(sp):
            sp.dma_start(k.xs[:], x.rearrange("b t d -> t b d")).then_inc(x_in, 16)
            sp.dma_start(k.g_x[:], g_xattn.partition_broadcast(P)).then_inc(g_in, 16)
            sp.dma_start(k.g_f[:], g_ffn.partition_broadcast(P)).then_inc(g_in, 16)
            sp.wait_ge(x_in, 16)

        @block.gpsimd
        def _(pool):
            nc.gpsimd.memset(k.ident[:], 0.0).then_inc(id_zero, 1)
            pool.wait_ge(id_zero, 1)
            nc.gpsimd.affine_select(out=k.ident[:], in_=k.ident[:], compare_op=ALU.not_equal, fill=1.0,
                                    base=0, pattern=[[-1, P]], channel_multiplier=1).then_inc(id_done, 1)
            pool.wait_ge(id_done, 1)

        @block.scalar
        def _(act):
            act.wait_ge(g_in, 32)
            nc.scalar.activation(k.tg_x[:], k.g_x[:], ACT.Tanh).then_inc(tanh_done, 1)
            nc.scalar.activation(k.tg_f[:], k.g_f[:], ACT.Tanh).then_inc(tanh_done, 1)
            act.wait_ge(tanh_done, 2)


def normalise(nc, k, name, rms=None, again=None):
    stats_done, var_done, root_done, rstd_done, xn_done, full, hi_done, lo_done, sq_done, sq_root, r_done, aux = (
        k.sem(f"{name}_{s}") for s in ("stats", "var", "root", "rstd", "xn", "full", "hi", "lo", "sq",
                                       "sqroot", "r", "aux"))
    with ExitStack() as ctx:
        stats = k.sb(f"{name}_stats", [T, B, 6], F32, ctx)
        root = k.sb(f"{name}_root", [T, B], F32, ctx)
        sums = k.sb(f"{name}_sums", [T, B], F32, ctx)
        sq = k.sb(f"{name}_sq", [T, 2, D], F32, ctx)
        eps = k.sb(f"{name}_eps", [T, 2], F32, ctx)
        eps_set = k.sem(f"{name}_epsset")
        with nc.Block() as block:
            @block.vector
            def _(dve):
                nc.vector.memset(eps[:, 0:1], LN_EPS).then_inc(eps_set, 1)
                nc.vector.memset(eps[:, 1:2], RMS_EPS).then_inc(eps_set, 1)
                for b in range(B):
                    nc.vector.bn_stats(stats[:, b, :], k.xs[:, b, :]).then_inc(stats_done, 1)
                for b in range(B):
                    dve.wait_ge(stats_done, b + 1)
                    nc.vector.bn_aggr(k.mv[:, b, :], stats[:, b, :]).then_inc(var_done, 1)
                dve.wait_ge(root_done, 1)
                nc.vector.reciprocal(k.rstd[:], root[:]).then_inc(rstd_done, 1)
                dve.wait_ge(rstd_done, 1)
                for b in range(B):
                    nc.vector.tensor_scalar(k.xn[:, b, :], k.xs[:, b, :], k.mv[:, b, 0:1], k.rstd[:, b:b + 1],
                                            ALU.subtract, ALU.mult).then_inc(xn_done, 1)
                if rms:
                    dve.wait_ge(sq_root, 1)
                    nc.vector.reciprocal(rms[0][:], rms[1][:]).then_inc(r_done, 1)
                    dve.wait_ge(r_done, 1)
                    for b in range(B):
                        nc.vector.tensor_scalar(k.xn[:, b, :], k.xn[:, b, :], rms[0][:, b:b + 1], None,
                                                ALU.mult).then_inc(xn_done, 1)
                if again:
                    for b in range(B):
                        dve.wait_ge(xn_done, b + 1)
                        nc.vector.bn_stats(stats[:, b, :], k.xn[:, b, :]).then_inc(stats_done, 1)
                    for b in range(B):
                        dve.wait_ge(stats_done, B + b + 1)
                        nc.vector.bn_aggr(again[0][:, b, :], stats[:, b, :]).then_inc(aux, 1)
                    dve.wait_ge(sq_root, 1)
                    nc.vector.reciprocal(again[1][:], root[:]).then_inc(r_done, 1)
                for g in range(NG):
                    dve.wait_ge(hi_done, g + 1)
                    bank = 2 * (g % 2)
                    nc.vector.tensor_tensor(k.xT[1][:, :, g * GT:(g + 1) * GT], k.ps[:, bank:bank + 2, :GT],
                                            k.xT[0][:, :, g * GT:(g + 1) * GT], ALU.subtract).then_inc(lo_done, 1)

            @block.scalar
            def _(act):
                act.wait_ge(var_done, B)
                act.wait_ge(eps_set, 2)
                nc.scalar.activation(root[:], k.mv[:, :, 1], ACT.Sqrt, bias=eps[:, 0:1]).then_inc(root_done, 1)
                if rms:
                    for b in range(B):
                        act.wait_ge(xn_done, b + 1)
                        if b >= 2:
                            act.wait_ge(sq_done, b - 1)
                        nc.scalar.activation(sq[:, b % 2, :], k.xn[:, b, :], ACT.Square,
                                             accum_out=sums[:, b:b + 1]).then_inc(sq_done, 1)
                    act.wait_ge(sq_done, B)
                    nc.scalar.activation(rms[1][:], sums[:], ACT.Sqrt, bias=eps[:, 1:2],
                                         scale=1.0 / D).then_inc(sq_root, 1)
                if again:
                    act.wait_ge(rstd_done, 1)
                    act.wait_ge(aux, B)
                    nc.scalar.activation(root[:], again[0][:, :, 1], ACT.Sqrt, bias=eps[:, 0:1]).then_inc(sq_root, 1)
                for g in range(NG):
                    act.wait_ge(full, g + 1)
                    bank = 2 * (g % 2)
                    nc.scalar.activation(k.xT[0][:, :, g * GT:(g + 1) * GT], k.ps[:, bank:bank + 2, :GT],
                                         ACT.Copy).then_inc(hi_done, 1)

            @block.tensor
            def _(pe):
                for g in range(NG):
                    pe.wait_ge(xn_done, (B if rms else 0) + GB * (g + 1))
                    if g >= 2:
                        pe.wait_ge(lo_done, g - 1)
                    bank = 2 * (g % 2)
                    for i in range(GB):
                        for t in range(KD):
                            last = nc.tensor.transpose(k.ps[:, bank + t, i * T:(i + 1) * T],
                                                       k.xn[:, GB * g + i, t * P:(t + 1) * P], k.ident[:T, :T])
                    last.then_inc(full, 1)


def load_square(nc, k, name, weights, scales, ctx):
    n = len(weights)
    raw = k.sb(f"{name}_raw", [P, n, KD, D], F32, ctx)
    parts = [[k.sb(f"{name}_w{i}_{p}", [P, KD, D], BF16, ctx) for p in ("hi", "lo")] for i in range(n)]
    w_in = [k.sem(f"{name}_in{i}") for i in range(n)]
    scaled, hi_done, lo_done = (k.sem(f"{name}_{s}") for s in ("scaled", "whi", "wlo"))
    with nc.Block() as block:
        @block.sync
        def _(sp):
            for i, w in enumerate(weights):
                sp.dma_start(raw[:, i], w.rearrange("(t p) n -> p t n", p=P)).then_inc(w_in[i], 16)

        @block.vector
        def _(dve):
            turned = 0
            for i in range(n):
                dve.wait_ge(w_in[i], 16)
                if scales[i] is not None:
                    nc.vector.tensor_scalar(raw[:, i], raw[:, i], scales[i], None, ALU.mult).then_inc(scaled, 1)
                    turned += 1
                    dve.wait_ge(scaled, turned)
                nc.vector.tensor_copy(parts[i][0][:], raw[:, i]).then_inc(hi_done, 1)
                dve.wait_ge(hi_done, i + 1)
                nc.vector.tensor_tensor(parts[i][1][:], raw[:, i], parts[i][0][:], ALU.subtract).then_inc(lo_done, 1)
            dve.wait_ge(lo_done, n)
    return parts


class Turn:

    def __init__(self, b, half, odd):
        self.b, self.half, self.odd = b, half, odd


def turn(b):
    return Turn(b, b // 2, b % 2)


def l0_attention(nc, k, ctxT, Wq, bq, Wk, bk, Wv, bv, Wo, bo):
    with ExitStack() as ctx:
        sb = lambda name, shape, dt: k.sb("a0_" + name, shape, dt, ctx)
        sem = lambda name: k.sem("a0_" + name)
        wq, wk, wv, wo = load_square(nc, k, "a0", [Wq, Wk, Wv, Wo], [None, None, None, k.tg_x[:, 0:1]], ctx)
        bias = sb("bias", [P, 3, KD], F32)
        bo_b = sb("bo", [T, D], F32)
        pair = sb("pair", [P, 2], F32)
        qf = sb("qf", [P, KD, N], F32)
        b_in, bo_in, pair_sum, pair_done, q_full, q_copied, bo_scaled = (
            sem(s) for s in ("b_in", "bo_in", "pairsum", "pair", "qfull", "qcopied", "boscaled"))

        with nc.Block() as block:
            @block.sync
            def _(sp):
                for i, v in enumerate((bq, bk, bv)):
                    sp.dma_start(bias[:, i, :], v).then_inc(b_in, 16)
                sp.dma_start(bo_b[:], bo.partition_broadcast(T)).then_inc(bo_in, 16)

            @block.vector
            def _(dve):
                nc.vector.tensor_reduce(pair[:], k.ident[:].rearrange("p (h two d) -> p two h d", two=2, d=DH),
                                        mybir.AxisListType.XY, ALU.add).then_inc(pair_sum, 1)
                dve.wait_ge(pair_sum, 1)
                nc.vector.tensor_scalar(pair[:], pair[:], DH ** -0.5, None, ALU.mult).then_inc(pair_done, 1)
                dve.wait_ge(bo_in, 16)
                nc.vector.tensor_scalar(bo_b[:], bo_b[:], k.tg_x[:T, 0:1], None, ALU.mult).then_inc(bo_scaled, 1)
                dve.wait_ge(bo_scaled, 1)
                dve.wait_ge(pair_done, 1)

            @block.tensor
            def _(pe):
                for g in range(NG):
                    for m in range(KD):
                        n = KD * g + m
                        if n >= 2:
                            pe.wait_ge(q_copied, n - 1)
                        three_products(nc, k.ps[:, n % 2, :GT],
                                       [(wq[0][:, t, m * P:(m + 1) * P], wq[1][:, t, m * P:(m + 1) * P]) for t in range(KD)],
                                       [(k.xT[0][:, t, g * GT:(g + 1) * GT], k.xT[1][:, t, g * GT:(g + 1) * GT])
                                        for t in range(KD)]).then_inc(q_full, 1)

            @block.scalar
            def _(act):
                act.wait_ge(b_in, 48)
                for g in range(NG):
                    for m in range(KD):
                        n = KD * g + m
                        act.wait_ge(q_full, n + 1)
                        nc.scalar.activation(qf[:, m, g * GT:(g + 1) * GT], k.ps[:, n % 2, :GT], ACT.Identity,
                                             bias=bias[:, 0, m:m + 1]).then_inc(q_copied, 1)
                act.wait_ge(q_copied, KD * NG)

        JJ = P // (2 * DH)
        NJ = KD * JJ
        stkK = sb("stkK", [98, 2, KD, JJ, S], BF16)
        stkQ = sb("stkQ", [98, 2, KD, JJ, QW], BF16)
        KS = sb("KS", [P, 2, 2, KD, S], BF16)
        QS = sb("QS", [P, 2, 2, KD, 2, T], BF16)
        ctxF = sb("ctxF", [P, 2, KD, S], F32)
        ctxH = sb("ctxH", [P, 2, KD, S], BF16)
        ctxL = sb("ctxL", [P, 2, KD, S], BF16)
        VW = 2 * DH + 1
        V = sb("V", [C, 2, SC, H, VW], BF16)
        PW = QW + 16
        Pf = sb("Pf", [C, 2, SC, QW], F32)
        Ph = sb("Ph", [C, 2, SC, PW], BF16)
        Pl = sb("Pl", [C, 2, SC, PW], BF16)
        mx = sb("mx", [T, 2, H], F32)
        cneg = sb("cneg", [H, 2, 2, T], BF16)
        rden = sb("rden", [T, 2, NJ], F32)
        osum = sb("osum", [T, 2, NJ, DH], F32)
        attn = sb("attn", [T, B, D], F32)
        psST = k.ps[:, 0:4, :].rearrange("p (u two) n -> p u (two n)", u=2)
        psMX = k.ps[:, 4:6, :]
        psPV = k.ps[:, 6, 0:NJ * VW].rearrange("p (h w) -> p h w", w=VW)
        psP = k.ps[:, 7, :]

        ones_set, passed = sem("ones"), sem("passed")
        ctx_in = [sem(f"ctxin{i}") for i in range(2)]
        kq_in = [sem(f"kqin{i}") for i in range(2)]
        c_in = [sem(f"cin{i}") for i in range(2)]
        (ctx_hi, ctx_lo, proj_full, part_hi, proj_free, q_hi, q_lo, st_full, exp_done, p_hi, p_lo, pv_full,
         mx_full, mx_red, c_hi, rden_done, pv_free, attn_done) = (sem(s) for s in (
             "ctxhi", "ctxlo", "projfull", "parthi", "projfree", "qhi", "qlo", "stfull", "expdone", "phi",
             "plo", "pvfull", "mxfull", "mxred", "chi", "rden", "pvfree", "attn"))
        COPIES = 3 * JJ
        KQ_IN = 2 * COPIES * 16
        TASKS = 5

        def passes(emit):
            emit(None, turn(0), turn(0), turn(0))
            emit(turn(0), turn(1), turn(2), turn(3))
            yield
            emit(turn(13), turn(14), turn(15), None)
            emit(turn(14), turn(15), None, None)
            emit(turn(15), None, None, None)

        def run(eng, emit):
            rest = passes(emit)
            next(rest)
            with eng.Fori(0, 6) as i:
                emit(Turn(2 * i + 1, i, 1), Turn(2 * i + 2, i + 1, 0), Turn(2 * i + 3, i + 1, 1), Turn(2 * i + 4, i + 2, 0))
                emit(Turn(2 * i + 2, i + 1, 0), Turn(2 * i + 3, i + 1, 1), Turn(2 * i + 4, i + 2, 0), Turn(2 * i + 5, i + 2, 1))
            for _ in rest:
                pass

        with nc.Block() as block:
            @block.sync
            def _(sp):
                def load(l):
                    if not isinstance(l.b, int) or l.b >= 2:
                        sp.wait_ge(ctx_lo, l.b - 1)
                    sp.sem_inc(passed, 1)
                    sp.dma_start(ctxF[:, l.odd], ctxT[bass.ds(l.b, 1)].rearrange("b (t p) s -> p (b t) s", p=P))\
                        .then_inc(ctx_in[l.odd], 16)

                def emit(b, n, w, l):
                    if b is None:
                        load(turn(0))
                        load(turn(1))
                        load(turn(2))
                    elif l is not None:
                        load(l)
                    if n is None:
                        return
                    o = n.odd
                    sp.wait_ge(q_lo, n.b * 2 + 2)
                    at_least(sp, st_full, n.b * NJ - NJ)
                    for jj in range(JJ):
                        for a, part in ((0, 0), (1, 0), (2, 1)):
                            sp.dma_start(stkQ[32 * a:32 * a + 32, o, :, jj, :],
                                         QS[32 * jj:32 * jj + 32, o, part].rearrange("p t h q -> p t (h q)"))\
                                .then_inc(kq_in[o], 16)
                    sp.wait_ge(proj_free, n.b * TASKS + 2)
                    for jj in range(JJ):
                        for a, part in ((0, 0), (1, 1), (2, 0)):
                            sp.dma_start(stkK[32 * a:32 * a + 32, o, :, jj, :], KS[32 * jj:32 * jj + 32, o, part])\
                                .then_inc(kq_in[o], 16)
                    sp.wait_ge(proj_free, n.b * TASKS + TASKS)
                    for part in range(2):
                        sp.dma_start(stkQ[96 + part:97 + part, o].rearrange("o t j (h q) -> o (t j h) q", q=T),
                                     cneg[:, o, part, :]).then_inc(c_in[o], 16)
                run(sp, emit)

            @block.tensor
            def _(pe):
                def scores(b, j):
                    if j == 0:
                        pe.wait_ge(kq_in[b.odd], b.half * KQ_IN + KQ_IN)
                        pe.wait_ge(c_in[b.odd], b.half * 32 + 32)
                    at_least(pe, exp_done, b.b * NJ + (j - 1))
                    for c in range(SC):
                        last = nc.tensor.matmul(psST[:C, j % 2, c * 256:c * 256 + QW],
                                                stkK[:, b.odd, j // JJ, j % JJ, c * C:(c + 1) * C],
                                                stkQ[:, b.odd, j // JJ, j % JJ, :], start=True, stop=True)
                    last.then_inc(st_full, 1)

                def values(b, j):
                    pe.wait_ge(p_lo, b.b * NJ + j + 1)
                    if j % JJ == 0:
                        at_least(pe, pv_free, b.b * 2 + j // JJ)
                    for h in range(2):
                        i = 0
                        for c in range(SC):
                            for part in (Ph, Pl):
                                last = nc.tensor.matmul(psPV[:, (2 * j + h) % NJ, :], part[:, j % 2, c, h * T:h * T + P],
                                                        V[:, b.odd, c, 2 * j + h, :], start=i == 0, stop=i == 2 * SC - 1)
                                i += 1
                    last.then_inc(pv_full, 1)

                def keys(n, m):
                    if m == 0:
                        pe.wait_ge(ctx_lo, n.b + 1)
                    at_least(pe, proj_free, n.b * TASKS + m)
                    three_products(nc, psP[:, :S],
                                   [(wk[0][:, t, m * P:(m + 1) * P], wk[1][:, t, m * P:(m + 1) * P]) for t in range(KD)],
                                   [(ctxH[:, n.odd, t, :], ctxL[:, n.odd, t, :]) for t in range(KD)]).then_inc(proj_full, 1)

                def vals(n, i):
                    pe.wait_ge(proj_free, n.b * TASKS + 2 + i)
                    for c in ((0, 1), (2,))[i]:
                        last = three_products(nc, psP[:C, (c % 2) * D:(c % 2 + 1) * D],
                                              [(ctxH[:, n.odd, t, c * C:(c + 1) * C], ctxL[:, n.odd, t, c * C:(c + 1) * C])
                                               for t in range(KD)],
                                              [(wv[0][:, t, :], wv[1][:, t, :]) for t in range(KD)])
                    last.then_inc(proj_full, 1)

                def maxima(n, j):
                    if j == 0:
                        pe.wait_ge(kq_in[n.odd], n.half * KQ_IN + KQ_IN)
                    at_least(pe, mx_red, n.b * NJ + j)
                    for h in range(2):
                        last = nc.tensor.matmul(psMX[:T, h, :S], stkQ[0:96, n.odd, j // JJ, j % JJ, h * T:(h + 1) * T],
                                                stkK[0:96, n.odd, j // JJ, j % JJ, :], start=True, stop=True)
                    last.then_inc(mx_full, 1)

                def turn_maxima(n):
                    pe.wait_ge(mx_red, n.b * NJ + NJ)
                    pe.wait_ge(proj_free, n.b * TASKS + 4)
                    nc.tensor.transpose(psP[:H, :T], mx[:, n.odd, :], k.ident[:T, :T]).then_inc(proj_full, 1)

                pe.wait_ge(ones_set, 5)

                def emit(b, n, w, l):
                    for s in range(NJ + 1):
                        if b is not None and s < NJ:
                            scores(b, s)
                        if b is not None and s > 0:
                            values(b, s - 1)
                        if n is not None:
                            if s < 2:
                                keys(n, s)
                            elif s < 4:
                                vals(n, s - 2)
                            elif s < 8:
                                maxima(n, 2 * (s - 4))
                                maxima(n, 2 * (s - 4) + 1)
                            else:
                                turn_maxima(n)
                run(pe, emit)

            @block.scalar
            def _(act):
                def emit(b, n, w, l):
                    for s in range(NJ):
                        if b is not None:
                            act.wait_ge(st_full, b.b * NJ + s + 1)
                            at_least(act, p_lo, b.b * NJ + (s - 1))
                            nc.scalar.activation(Pf[:, s % 2], psST[:C, s % 2, 0:SC * 256].rearrange(
                                "p (c n) -> p c n", c=SC)[:, :, :QW], ACT.Exp).then_inc(exp_done, 1)
                        if n is None:
                            continue
                        if s < 2:
                            if s == 0:
                                at_least(act, kq_in[n.odd], n.half * KQ_IN)
                            act.wait_ge(proj_full, n.b * TASKS + s + 1)
                            nc.scalar.activation(KS[:, n.odd, 0, s, :], psP[:, :S], ACT.Identity,
                                                 bias=bias[:, 1, s:s + 1]).then_inc(part_hi, 1)
                        elif s < 4:
                            if s == 2:
                                at_least(act, pv_full, n.b * NJ - NJ)
                            act.wait_ge(proj_full, n.b * TASKS + s + 1)
                            c0, nc_ = ((0, 2), (2, 1))[s - 2]
                            nc.scalar.activation(V[:, n.odd, c0:c0 + nc_, :, 0:DH],
                                                 psP[:C, 0:nc_ * D].rearrange("p (c h d) -> p c h d", c=nc_, d=DH),
                                                 ACT.Copy).then_inc(part_hi, 1)
                run(act, emit)

            @block.gpsimd
            def _(pool):
                nc.gpsimd.memset(Pl[:], 0.0).then_inc(ones_set, 1)
                pool.wait_ge(ones_set, 1)

                def ctx_low(w):
                    pool.wait_ge(ctx_hi, w.b + 1)
                    nc.gpsimd.tensor_tensor(ctxL[:, w.odd], ctxF[:, w.odd], ctxH[:, w.odd], ALU.subtract).then_inc(ctx_lo, 1)

                def emit(b, n, w, l):
                    if b is None:
                        ctx_low(turn(0))
                        ctx_low(turn(1))
                        return
                    for s in range(NJ):
                        pool.wait_ge(p_hi, b.b * NJ + s + 1)
                        at_least(pool, pv_full, b.b * NJ + (s - 1))
                        nc.gpsimd.tensor_tensor(Pl[:, s % 2, :, :QW], Pf[:, s % 2], Ph[:, s % 2, :, :QW],
                                                ALU.subtract).then_inc(p_lo, 1)
                    if w is not None:
                        ctx_low(w)
                run(pool, emit)

            @block.vector
            def _(dve):
                nc.vector.memset(Ph[:], 0.0).then_inc(ones_set, 1)
                nc.vector.memset(V[:], 1.0).then_inc(ones_set, 1)
                nc.vector.memset(stkK[96:98], 1.0).then_inc(ones_set, 1)
                nc.vector.memset(mx[:], 0.0).then_inc(ones_set, 1)
                dve.wait_ge(ones_set, 5)

                def ctx_high(w):
                    dve.wait_ge(ctx_in[w.odd], w.half * 16 + 16)
                    at_least(dve, proj_full, w.b * TASKS - 2 * TASKS + 4)
                    nc.vector.tensor_copy(ctxH[:, w.odd], ctxF[:, w.odd]).then_inc(ctx_hi, 1)

                def queries(n):
                    at_least(dve, kq_in[n.odd], n.half * KQ_IN)
                    q = qf[:, :, bass.ds(n.b * T, T)]
                    for h in range(2):
                        nc.vector.tensor_scalar(QS[:, n.odd, 0, :, h, :], q, pair[:, h:h + 1], None,
                                                ALU.mult).then_inc(q_hi, 1)
                    for h in range(2):
                        dve.wait_ge(q_hi, n.b * 2 + h + 1)
                        nc.vector.scalar_tensor_tensor(QS[:, n.odd, 1, :, h, :], q, pair[:, h:h + 1],
                                                       QS[:, n.odd, 0, :, h, :], ALU.mult, ALU.subtract).then_inc(q_lo, 1)

                def reduce(n, j):
                    if j == 0:
                        at_least(dve, proj_full, n.b * TASKS - TASKS)
                    dve.wait_ge(mx_full, n.b * NJ + j + 1)
                    nc.vector.reduce_max(mx[:, n.odd, 2 * j:2 * j + 2], psMX[:T, :, :S], AX).then_inc(mx_red, 1)

                def minus_maxima(n):
                    at_least(dve, c_in[n.odd], n.half * 32)
                    dve.wait_ge(proj_full, n.b * TASKS + TASKS)
                    nc.vector.tensor_scalar(cneg[:, n.odd, 0, :], psP[:H, :T], -1.0, None, ALU.mult).then_inc(c_hi, 1)
                    dve.wait_ge(c_hi, n.b + 1)
                    nc.vector.scalar_tensor_tensor(cneg[:, n.odd, 1, :], psP[:H, :T], -1.0, cneg[:, n.odd, 0, :],
                                                   ALU.mult, ALU.subtract).then_inc(proj_free, 1)

                def finish(b, half):
                    dve.wait_ge(pv_full, b.b * NJ + JJ * (half + 1))
                    at_least(dve, attn_done, b.b * 2 + half)
                    nc.vector.reciprocal(rden[:, half, :], psPV[:T, :, 2 * DH]).then_inc(rden_done, 1)
                    nc.vector.tensor_copy(osum[:, half], psPV[:T, :, 0:DH]).then_inc(rden_done, 1)
                    dve.wait_ge(rden_done, b.b * 4 + 2 * half + 2)
                    nc.vector.tensor_tensor(osum[:, half], psPV[:T, :, DH:2 * DH], osum[:, half],
                                            ALU.add).then_inc(pv_free, 1)
                    dve.wait_ge(pv_free, b.b * 2 + half + 1)
                    nc.vector.tensor_tensor(
                        attn[:, bass.ds(b.b, 1), half * P:(half + 1) * P].rearrange("p o (h d) -> p (o h) d", d=DH),
                        osum[:, half], rden[:, half, :].unsqueeze(2).broadcast_to([T, NJ, DH]), ALU.mult).then_inc(attn_done, 1)

                def emit(b, n, w, l):
                    if b is None:
                        ctx_high(turn(0))
                        ctx_high(turn(1))
                    if n is not None:
                        queries(n)
                    for s in range(NJ + 1):
                        if b is not None and s < NJ:
                            dve.wait_ge(exp_done, b.b * NJ + s + 1)
                            at_least(dve, pv_full, b.b * NJ + (s - 1))
                            nc.vector.tensor_copy(Ph[:, s % 2, :, :QW], Pf[:, s % 2]).then_inc(p_hi, 1)
                        if b is not None and s == 5:
                            finish(b, 0)
                        if n is not None:
                            if s < 2:
                                dve.wait_ge(part_hi, n.b * 4 + s + 1)
                                nc.vector.scalar_tensor_tensor(KS[:, n.odd, 1, s, :], psP[:, :S], bias[:, 1, s:s + 1],
                                                               KS[:, n.odd, 0, s, :], ALU.add, ALU.subtract).then_inc(proj_free, 1)
                            elif s < 4:
                                dve.wait_ge(part_hi, n.b * 4 + s + 1)
                                c0, nc_ = ((0, 2), (2, 1))[s - 2]
                                nc.vector.tensor_tensor(V[:, n.odd, c0:c0 + nc_, :, DH:2 * DH],
                                                        psP[:C, 0:nc_ * D].rearrange("p (c h d) -> p c h d", c=nc_, d=DH),
                                                        V[:, n.odd, c0:c0 + nc_, :, 0:DH], ALU.subtract).then_inc(proj_free, 1)
                            elif s < 8:
                                reduce(n, 2 * (s - 4))
                                reduce(n, 2 * (s - 4) + 1)
                        if s == 6 and w is not None and b is not None:
                            ctx_high(w)
                    if b is not None:
                        finish(b, 1)
                    if n is not None:
                        minus_maxima(n)
                run(dve, emit)

        output_projection(nc, k, "a0", attn, bias[:, 2, :], wo, bo_b, ctx)


def output_projection(nc, k, name, attn, bv, wo, bo_b, ctx):
    aT = [k.sb(f"{name}_aT_{p}", [P, 2, KD, GT], BF16, ctx) for p in ("hi", "lo")]
    t_full, hi_done, lo_done, y_full, y_used, sum_done = (
        k.sem(f"{name}_o_{s}") for s in ("tfull", "hi", "lo", "yfull", "yused", "sum"))
    with nc.Block() as block:
        @block.tensor
        def _(pe):
            def turned(g):
                if g >= 2:
                    pe.wait_ge(lo_done, KD * (g - 1))
                for i in range(GB):
                    for t in range(KD):
                        last = nc.tensor.transpose(k.ps[:, 2 * (g % 2) + t, i * T:(i + 1) * T],
                                                   attn[:, GB * g + i, t * P:(t + 1) * P], k.ident[:T, :T])
                last.then_inc(t_full, 1)
            turned(0)
            for g in range(NG):
                if g + 1 < NG:
                    turned(g + 1)
                pe.wait_ge(lo_done, KD * (g + 1))
                for i in range(GB):
                    n = GB * g + i
                    if n >= 4:
                        pe.wait_ge(y_used, n - 3)
                    three_products(nc, k.ps[:T, 4 + n % 4, :D],
                                   [(aT[0][:, g % 2, t, i * T:(i + 1) * T], aT[1][:, g % 2, t, i * T:(i + 1) * T])
                                    for t in range(KD)],
                                   [(wo[0][:, t, :], wo[1][:, t, :]) for t in range(KD)]).then_inc(y_full, 1)

        @block.scalar
        def _(act):
            for g in range(NG):
                act.wait_ge(t_full, g + 1)
                if g >= 2:
                    act.wait_ge(y_full, GB * (g - 1))
                for t in range(KD):
                    nc.scalar.activation(aT[0][:, g % 2, t, :], k.ps[:, 2 * (g % 2) + t, :GT], ACT.Identity,
                                         bias=bv[:, t:t + 1]).then_inc(hi_done, 1)

        @block.vector
        def _(dve):
            def low(g):
                for t in range(KD):
                    dve.wait_ge(hi_done, KD * g + t + 1)
                    nc.vector.scalar_tensor_tensor(aT[1][:, g % 2, t, :], k.ps[:, 2 * (g % 2) + t, :GT], bv[:, t:t + 1],
                                                   aT[0][:, g % 2, t, :], ALU.add, ALU.subtract).then_inc(lo_done, 1)
            low(0)
            for g in range(NG):
                if g + 1 < NG:
                    low(g + 1)
                for i in range(GB):
                    n = GB * g + i
                    dve.wait_ge(y_full, n + 1)
                    nc.vector.tensor_tensor(k.xs[:, n, :], k.ps[:T, 4 + n % 4, :D], k.xs[:, n, :],
                                            ALU.add).then_inc(y_used, 1)
                    dve.wait_ge(y_used, n + 1)
                    nc.vector.tensor_tensor(k.xs[:, n, :], k.xs[:, n, :], bo_b[:], ALU.add).then_inc(sum_done, 1)
            dve.wait_ge(sum_done, B)




def linker(engine, sem):
    count = [0]

    def link(ins):
        count[0] += 1
        ins.then_inc(sem, 1)
        engine.wait_ge(sem, count[0])
    return link


def skewed(eng, emit):
    PEEL = 4
    for r in range(PEEL):
        emit(turn(r), turn(r - 1) if r >= 1 else None, turn(r - 2) if r >= 2 else None)
    with eng.Fori(0, (B - PEEL) // 2) as i:
        emit(Turn(2 * i + 4, i + 2, 0), Turn(2 * i + 3, i + 1, 1), Turn(2 * i + 2, i + 1, 0))
        emit(Turn(2 * i + 5, i + 2, 1), Turn(2 * i + 4, i + 2, 0), Turn(2 * i + 3, i + 1, 1))
    emit(None, turn(B - 1), turn(B - 2))
    emit(None, None, turn(B - 1))


def route(nc, k, name, router_dram, E, gate, eps, factor, ctx, rms=None, affine=None):
    EP = max(E, 8)
    sb = lambda n_, shape, dt: k.sb(f"{name}_r_{n_}", shape, dt, ctx)
    sem = lambda n_: k.sem(f"{name}_r_{n_}")
    rt = sb("rt", [P, KD, 2 * E], F32)
    rp = [sb(f"rt{p}", [P, KD, E], BF16) for p in ("hi", "lo")]
    raw = sb("raw", [P, KD, E], F32)
    iota_i, iota = sb("iotai", [T, EP], mybir.dt.int32), sb("iota", [T, EP], F32)
    L = sb("L", [T, B, EP], F32)
    red, m8, idx, idxf = sb("red", [T, B], F32), sb("m8", [T, B, 8], F32), sb("idx", [T, B, 8], U32), sb("idxf", [T, B, 2], F32)
    pick = sb("pick", [T, 2, B, EP], F32)
    ones = sb("ones", [P, T], F32)
    sums = sb("sums", [T, 2 * E], F32)
    r_in, iota_done, parts_done, sums_full, full, exp_ready, exp_done, step = (
        sem(s) for s in ("in", "iota", "parts", "sumsfull", "full", "expready", "exp", "step"))
    over = lambda ap: ap.unsqueeze(2).broadcast_to([T, B, EP])
    logits = k.ps[:T, 0, 0:B * E].rearrange("p (b e) -> p b e", e=E)
    with nc.Block() as block:
        @block.sync
        def _(sp):
            sp.dma_start(raw[:], router_dram).then_inc(r_in, 16)

        @block.gpsimd
        def _(pool):
            nc.gpsimd.iota(iota_i[:], pattern=[[1, EP]], base=0, channel_multiplier=0).then_inc(iota_done, 1)

        @block.tensor
        def _(pe):
            pe.wait_ge(parts_done, 1)
            if affine:
                for t in range(KD):
                    last = nc.tensor.matmul(k.ps[:T, 1, 0:2 * E], ones[:], rt[:, t, :], start=t == 0, stop=t == KD - 1)
                last.then_inc(sums_full, 1)
            for b in range(B):
                last = three_products(nc, logits[:, b, :],
                                      [(k.xT[0][:, t, b * T:(b + 1) * T], k.xT[1][:, t, b * T:(b + 1) * T]) for t in range(KD)],
                                      [(rp[0][:, t, :], rp[1][:, t, :]) for t in range(KD)])
            last.then_inc(full, 1)

        @block.scalar
        def _(act):
            act.wait_ge(exp_ready, 1)
            nc.scalar.activation(L[:], L[:], ACT.Exp).then_inc(exp_done, 1)

        @block.vector
        def _(dve):
            link = linker(dve, step)
            tt, ts = nc.vector.tensor_tensor, nc.vector.tensor_scalar
            dve.wait_ge(r_in, 16)
            dve.wait_ge(iota_done, 1)
            link(nc.vector.tensor_copy(iota[:], iota_i[:]))
            if affine:
                scale, offset, mean, rstd = affine
                link(nc.vector.memset(ones[:], 1.0))
                for t in range(KD):
                    link(ts(rt[:, t, 0:E], raw[:, t, :], scale[:, t:t + 1], None, ALU.mult))
                    link(ts(rt[:, t, E:], raw[:, t, :], offset[:, t:t + 1], None, ALU.mult))
            else:
                link(nc.vector.tensor_copy(rt[:, :, 0:E], raw[:]))
            link(nc.vector.tensor_copy(rp[0][:], rt[:, :, 0:E]))
            tt(rp[1][:], rt[:, :, 0:E], rp[0][:], ALU.subtract).then_inc(parts_done, 1)
            if EP > E:
                link(nc.vector.memset(L[:], -1.0))
            dve.wait_ge(full, 1)
            l = L[:, :, 0:E]
            over_e = lambda ap: ap.unsqueeze(2).broadcast_to([T, B, E])
            if affine:
                dve.wait_ge(sums_full, 1)
                link(nc.vector.tensor_copy(sums[:], k.ps[:T, 1, 0:2 * E]))
                cols = lambda c: sums[:, c:c + E].unsqueeze(1).broadcast_to([T, B, E])
                link(tt(pick[:, 0, :, 0:E], cols(0), over_e(mean), ALU.mult))
                link(tt(l, logits, pick[:, 0, :, 0:E], ALU.subtract))
                link(tt(l, l, over_e(rstd), ALU.mult))
                link(tt(l, l, cols(E), ALU.add))
            else:
                link(tt(l, logits, over_e(rms[:]), ALU.mult))
            link(nc.vector.reduce_max(red[:], l, AX))
            tt(l, l, over_e(red[:]), ALU.subtract).then_inc(exp_ready, 1)
            dve.wait_ge(exp_done, 1)
            link(nc.vector.reduce_sum(red[:], l, AX))
            link(nc.vector.reciprocal(red[:], red[:]))
            link(tt(l, l, over_e(red[:]), ALU.mult))
            if EP > E:
                link(nc.vector.memset(L[:, :, E:], -1.0))
            for b in range(B):
                last = nc.vector.max(m8[:, b, :], L[:, b, :])
            link(last)
            for b in range(B):
                last = nc.vector.max_index(idx[:, b, :], m8[:, b, :], L[:, b, :])
            link(last)
            link(nc.vector.tensor_copy(idxf[:], idx[:, :, 0:2]))
            link(tt(red[:], m8[:, :, 0], m8[:, :, 1], ALU.add))
            link(ts(red[:], red[:], eps, None, ALU.add))
            link(nc.vector.reciprocal(red[:], red[:]))
            link(ts(red[:], red[:], factor, None, ALU.mult))
            for i in range(2):
                link(tt(pick[:, i], iota[:].unsqueeze(1).broadcast_to([T, B, EP]), over(idxf[:, :, i]), ALU.is_equal))
                link(tt(pick[:, i], pick[:, i], over(m8[:, :, i]), ALU.mult))
            link(tt(pick[:, 0], pick[:, 0], pick[:, 1], ALU.add))
            link(tt(gate[:, :, 0:E], pick[:, 0, :, 0:E], over_e(red[:]), ALU.mult))


def l0_experts(nc, k, a):
    with ExitStack() as ctx:
        sb = lambda name, shape, dt: k.sb("f0_" + name, shape, dt, ctx)
        sem = lambda name: k.sem("f0_" + name)
        rms_inv, rms = sb("rmsinv", [T, B], F32), sb("rms", [T, B], F32)
        normalise(nc, k, "n1", rms=(rms_inv, rms))
        gate = sb("gate", [T, B, E0 + E0S], F32)
        with ExitStack() as rctx:
            route(nc, k, "f0", a["F0_router_w"].rearrange("(t p) e -> p t e", p=P), E0, gate, L0_GATE_EPS,
                  k.tg_f[:T, 0:1], rctx, rms=rms)

        raw1 = sb("raw1", [P, 2, KD, HID], F32)
        raw2 = sb("raw2", [P, 2, HM, D], F32)
        w1 = [sb(f"w1{p}", [P, 2, KD, HID], BF16) for p in ("hi", "lo")]
        w2 = [sb(f"w2{p}", [P, 2, HM, D], BF16) for p in ("hi", "lo")]
        rw = sb("rw", [P, E0 + E0S, KD], F32)
        hf = sb("hf", [P, 2, HM, GT], F32)
        hh = sb("hh", [P, 2, HM, GT], BF16)
        hl = sb("hl", [P, 2, HM, GT], BF16)
        w_in = [sem("win0"), sem("win1")]
        rw_in, gate_set, w_hi, w1_lo, w2_lo, up_full, act_done, h_hi, h_lo, y_full, y_used = (
            sem(s) for s in ("rwin", "gateset", "whi", "w1lo", "w2lo", "upfull", "act", "hhi", "hlo", "yfull", "yused"))
        passed = sem("passed")
        UP, DOWN = NG * HM, NG * GB
        FREE_ACT, FREE_HID, FREE_Y, FREE_W1, FREE_W2, DONE_Y = HM, 2 * HM, DOWN, 2 * KD, 2, DOWN

        def experts(eng, emit):
            with eng.Fori(0, E0 // 2) as i:
                emit(2 * i, i, 0, 0, 2 * i)
                emit(2 * i + 1, i, 1, 0, 2 * i + 1)
            for s in range(E0S):
                emit(E0 + s, (E0 + s) // 2, s % 2, 1, s)

        with nc.Block() as block:
            @block.sync
            def _(sp):
                sp.dma_start(rw[:, 0:E0, :], a["F0_rms_w"]).then_inc(rw_in, 16)
                sp.dma_start(rw[:, E0:, :], a["F0_rms_w_s"]).then_inc(rw_in, 16)

                def emit(e, half, odd, shared, i):
                    s1, s2 = ((a["F0_w1"], a["F0_w2"]), (a["F0_w1_s"], a["F0_w2_s"]))[shared]
                    sp.wait_ge(w1_lo, FREE_W1 + KD * (e - 1))
                    sp.sem_inc(passed, 1)
                    sp.wait_ge(w2_lo, FREE_W2 + e - 1)
                    sp.sem_inc(passed, 1)
                    sp.dma_start(raw1[:, odd], s1[bass.ds(i, 1)].rearrange("e (t p) n -> p (e t) n", p=P))\
                        .then_inc(w_in[odd], 16)
                    sp.dma_start(raw2[:, odd], s2[bass.ds(i, 1)].rearrange("e (t p) n -> p (e t) n", p=P))\
                        .then_inc(w_in[odd], 16)
                experts(sp, emit)

            @block.gpsimd
            def _(pool):
                pool.sem_inc(w2_lo, FREE_W2)

                def emit(e, half, odd, shared, i):
                    pool.wait_ge(w_hi, (KD + 1) * (e + 1))
                    nc.gpsimd.tensor_tensor(w2[1][:, odd], raw2[:, odd], w2[0][:, odd], ALU.subtract).then_inc(w2_lo, 1)
                experts(pool, emit)

            @block.tensor
            def _(pe):
                pe.sem_inc(y_full, DONE_Y)

                def emit(e, half, odd, shared, i):
                    pe.wait_ge(w1_lo, FREE_W1 + KD * (e + 1))
                    pe.wait_ge(w2_lo, FREE_W2 + e + 1)
                    for g in range(NG):
                        for m in range(HM):
                            pe.wait_ge(act_done, FREE_ACT + e * UP + g * HM + m + 1 - HM)
                            three_products(nc, k.ps[:, m, :GT],
                                           [(w1[0][:, odd, t, m * P:(m + 1) * P], w1[1][:, odd, t, m * P:(m + 1) * P])
                                            for t in range(KD)],
                                           [(k.xT[0][:, t, g * GT:(g + 1) * GT], k.xT[1][:, t, g * GT:(g + 1) * GT])
                                            for t in range(KD)]).then_inc(up_full, 1)
                        for m in range(HM):
                            pe.wait_ge(h_lo, FREE_HID + e * UP + g * HM + m + 1)
                            for q in range(GB):
                                if m == 0:
                                    pe.wait_ge(y_used, FREE_Y + e * DOWN + g * GB + q + 1 - GB)
                                last = three_products(nc, k.ps[:T, 4 + q, :D],
                                                      [(hh[:, g % 2, m, q * T:(q + 1) * T], hl[:, g % 2, m, q * T:(q + 1) * T])],
                                                      [(w2[0][:, odd, m, :], w2[1][:, odd, m, :])],
                                                      first=m == 0, last=m == HM - 1)
                                if m == HM - 1:
                                    last.then_inc(y_full, 1)
                experts(pe, emit)

            @block.scalar
            def _(act):
                act.sem_inc(act_done, FREE_ACT)

                def emit(e, half, odd, shared, i):
                    for g in range(NG):
                        for m in range(HM):
                            n = g * HM + m
                            act.wait_ge(up_full, e * UP + n + 1)
                            act.wait_ge(h_lo, FREE_HID + e * UP + n + 1 - 2 * HM)
                            nc.scalar.activation(hf[:, g % 2, m, :], k.ps[:, m, :GT], ACT.Silu).then_inc(act_done, 1)
                experts(act, emit)

            @block.vector
            def _(dve):
                dve.sem_inc(h_lo, FREE_HID)
                dve.sem_inc(y_used, FREE_Y)
                dve.sem_inc(w1_lo, FREE_W1)
                for s in range(E0S):
                    for b in range(B):
                        last = nc.vector.tensor_copy(gate[:, b, E0 + s:E0 + s + 1], k.tg_f[:T, 0:1])
                last.then_inc(gate_set, 1)
                dve.wait_ge(gate_set, 1)
                dve.wait_ge(rw_in, 32)

                def split(e, half, odd):
                    dve.wait_ge(w_in[odd], half * 32 + 32)
                    dve.wait_ge(y_full, DONE_Y * e)
                    scale = lambda t: rw[:, bass.ds(e, 1), t]
                    for t in range(KD):
                        nc.vector.tensor_scalar(w1[0][:, odd, t, :], raw1[:, odd, t, :], scale(t), None, ALU.mult).then_inc(w_hi, 1)
                    nc.vector.tensor_copy(w2[0][:, odd], raw2[:, odd]).then_inc(w_hi, 1)
                    for t in range(KD):
                        dve.wait_ge(w_hi, (KD + 1) * e + t + 1)
                        nc.vector.scalar_tensor_tensor(w1[1][:, odd, t, :], raw1[:, odd, t, :], scale(t),
                                                       w1[0][:, odd, t, :], ALU.mult, ALU.subtract).then_inc(w1_lo, 1)
                split(0, 0, 0)

                def emit(e, half, odd, shared, i):
                    for g in range(NG):
                        for m in range(HM):
                            n = g * HM + m
                            dve.wait_ge(act_done, FREE_ACT + e * UP + n + 1)
                            dve.wait_ge(y_full, DONE_Y + e * DOWN + g * GB + GB - 2 * GB)
                            nc.vector.tensor_copy(hh[:, g % 2, m, :], hf[:, g % 2, m, :]).then_inc(h_hi, 1)
                            dve.wait_ge(h_hi, e * UP + n + 1)
                            nc.vector.tensor_tensor(hl[:, g % 2, m, :], hf[:, g % 2, m, :], hh[:, g % 2, m, :],
                                                    ALU.subtract).then_inc(h_lo, 1)
                        for q in range(GB):
                            dve.wait_ge(y_full, DONE_Y + e * DOWN + g * GB + q + 1)
                            dve.wait_ge(y_used, FREE_Y + e * DOWN - DOWN + g * GB + q + 1)
                            nc.vector.scalar_tensor_tensor(k.xs[:, GB * g + q, :], k.ps[:T, 4 + q, :D],
                                                           gate[:, GB * g + q, bass.ds(e, 1)], k.xs[:, GB * g + q, :],
                                                           ALU.mult, ALU.add).then_inc(y_used, 1)
                        if g == 0 and not (isinstance(e, int) and e == E0 + E0S - 1):
                            split(e + 1, half + odd, 1 - odd)
                experts(dve, emit)


def l1_attention(nc, k, a):
    with ExitStack() as ctx:
        sb = lambda name, shape, dt: k.sb("a1_" + name, shape, dt, ctx)
        sem = lambda name: k.sem("a1_" + name)
        normalise(nc, k, "n2")
        wq, wk, wv, wo = load_square(nc, k, "a1", [a["L1_Wq"], a["L1_Wk"], a["L1_Wv"], a["L1_Wo"]],
                                     [None, None, None, k.tg_x[:, 1:2]], ctx)
        bias = sb("bias", [P, 3, KD], F32)
        bk2 = sb("bk2", [P, KD, 2], BF16)
        bo_b = sb("bo", [T, D], F32)
        qT = [sb(f"qT{p}", [P, KD, N], BF16) for p in ("hi", "lo")]
        qkT = [sb(f"qkT{p}", [P, KD, N], BF16) for p in ("hi", "lo")]
        qbk = sb("qbk", [T, B], F32)
        qbk2 = sb("qbk2", [T, B, 2], F32)
        b_in, bo_in, small, full, hi_done, lo_done, bk_full = (
            sem(s) for s in ("bin", "boin", "small", "qfull", "qhi", "qlo", "bkfull"))
        cols = lambda g: slice(g * GT, (g + 1) * GT)

        with nc.Block() as block:
            @block.sync
            def _(sp):
                for i, v in enumerate((a["L1_bq"], a["L1_bk"], a["L1_bv"])):
                    sp.dma_start(bias[:, i, :], v).then_inc(b_in, 16)
                sp.dma_start(bo_b[:], a["L1_bo"].partition_broadcast(T)).then_inc(bo_in, 16)

            @block.tensor
            def _(pe):
                for s, (w, src) in enumerate(((wq, k.xT), (wk, qT))):
                    for g in range(NG):
                        for m in range(KD):
                            n = (s * NG + g) * KD + m
                            if n >= 4:
                                pe.wait_ge(lo_done, n - 3)
                            if s == 1:
                                pe.wait_ge(lo_done, (g + 1) * KD)
                            three_products(nc, k.ps[:, n % 4, :GT],
                                           [(w[0][:, t, m * P:(m + 1) * P], w[1][:, t, m * P:(m + 1) * P]) for t in range(KD)],
                                           [(src[0][:, t, cols(g)], src[1][:, t, cols(g)]) for t in range(KD)]).then_inc(full, 1)
                pe.wait_ge(small, 2)
                for b in range(B):
                    for t in range(KD):
                        for i in range(2):
                            last = nc.tensor.matmul(k.ps[:T, 4, 2 * b:2 * b + 2], qT[i][:, t, b * T:(b + 1) * T],
                                                    bk2[:, t, :], start=t == 0 and i == 0, stop=t == KD - 1 and i == 1)
                last.then_inc(bk_full, 1)

            @block.scalar
            def _(act):
                act.wait_ge(b_in, 48)
                for s, dst in enumerate((qT, qkT)):
                    for g in range(NG):
                        for m in range(KD):
                            n = (s * NG + g) * KD + m
                            act.wait_ge(full, n + 1)
                            nc.scalar.activation(dst[0][:, m, cols(g)], k.ps[:, n % 4, :GT], ACT.Identity,
                                                 bias=bias[:, 0, m:m + 1] if s == 0 else 0.0).then_inc(hi_done, 1)

            @block.vector
            def _(dve):
                dve.wait_ge(b_in, 48)
                nc.vector.tensor_copy(bk2[:, :, 0], bias[:, 1, :]).then_inc(small, 1)
                dve.wait_ge(small, 1)
                nc.vector.tensor_tensor(bk2[:, :, 1], bias[:, 1, :], bk2[:, :, 0], ALU.subtract).then_inc(small, 1)
                dve.wait_ge(bo_in, 16)
                nc.vector.tensor_scalar(bo_b[:], bo_b[:], k.tg_x[:T, 1:2], None, ALU.mult).then_inc(small, 1)
                for s, dst in enumerate((qT, qkT)):
                    for g in range(NG):
                        for m in range(KD):
                            n = (s * NG + g) * KD + m
                            dve.wait_ge(hi_done, n + 1)
                            if s == 0:
                                last = nc.vector.scalar_tensor_tensor(dst[1][:, m, cols(g)], k.ps[:, n % 4, :GT],
                                                                      bias[:, 0, m:m + 1], dst[0][:, m, cols(g)],
                                                                      ALU.add, ALU.subtract)
                            else:
                                last = nc.vector.tensor_tensor(dst[1][:, m, cols(g)], k.ps[:, n % 4, :GT],
                                                               dst[0][:, m, cols(g)], ALU.subtract)
                            last.then_inc(lo_done, 1)
                dve.wait_ge(bk_full, 1)
                nc.vector.tensor_copy(qbk2[:], k.ps[:T, 4, 0:2 * B].rearrange("p (b two) -> p b two", two=2)).then_inc(small, 1)
                dve.wait_ge(small, 4)
                nc.vector.tensor_tensor(qbk[:], qbk2[:, :, 0], qbk2[:, :, 1], ALU.add).then_inc(small, 1)
                dve.wait_ge(small, 5)
                dve.wait_ge(lo_done, 2 * NG * KD)

        cT = sb("cT", [P, 2, KD, S], F32)
        cTp = [sb(f"cT{p}", [P, 2, KD, S], BF16) for p in ("hi", "lo")]
        cR = sb("cR", [C, 2, SC, D], F32)
        cRp = [sb(f"cR{p}", [C, 2, SC, D], BF16) for p in ("hi", "lo")]
        pr = sb("pr", [T, 2, S], F32)
        pT = [sb(f"pT{p}", [C, 2, SC, T], BF16) for p in ("hi", "lo")]
        mT = [sb(f"mT{p}", [P, KD, N], BF16) for p in ("hi", "lo")]
        scale_t = sb("scale", [T, 1], F32)
        small_t = sb("small", [T, 2, 4], F32)
        c_in = [sem("cin0"), sem("cin1")]
        (ct_hi, ct_lo, cr_hi, cr_lo, s_full, bias_step, p_done, pn_done, t_full, pt_hi, pt_lo, m_full, m_hi, m_lo) = (
            sem(s) for s in ("cthi", "ctlo", "crhi", "crlo", "sfull", "biasstep", "pdone", "pndone", "tfull", "pthi",
                             "ptlo", "mfull", "mhi", "mlo"))
        SCALE = D ** -0.5
        pn_done_r, scale_set, passed = sem("rsum"), sem("scaleset"), sem("passed")
        row = lambda b: bass.ds(b.b * T, T)
        one = lambda ap, b: ap[:, bass.ds(b.b, 1)]

        with nc.Block() as block:
            @block.sync
            def _(sp):
                with sp.Fori(0, B // 2) as i:
                    for o in range(2):
                        b = 2 * i + o
                        sp.wait_ge(ct_lo, b + 1)
                        sp.sem_inc(passed, 1)
                        sp.dma_start(cT[:, o], a["ctxT"][bass.ds(b, 1)].rearrange("b (t p) s -> p (b t) s", p=P)).then_inc(c_in[o], 16)
                        sp.wait_ge(cr_lo, b + 1)
                        sp.sem_inc(passed, 1)
                        sp.dma_start(cR[:, o], a["ctx"][bass.ds(b, 1)].rearrange("b (c p) d -> p (b c) d", p=C)).then_inc(c_in[o], 16)

            @block.gpsimd
            def _(pool):
                pool.sem_inc(cr_lo, 2)

                def emit(s, t, m):
                    if s is None:
                        return
                    pool.wait_ge(cr_hi, s.b + 1)
                    pool.wait_ge(m_full, 3 + s.b - 1)
                    nc.gpsimd.tensor_tensor(cRp[1][:, s.odd], cR[:, s.odd], cRp[0][:, s.odd],
                                            ALU.subtract).then_inc(cr_lo, 1)
                skewed(pool, emit)

            @block.tensor
            def _(pe):
                pe.sem_inc(m_full, 3)

                def emit(s, t, m):
                    if s is not None:
                        pe.wait_ge(ct_lo, s.b + 3)
                        at_least(pe, p_done, s.b - 1)
                        three_products(nc, k.ps[:T, s.odd, :S],
                                       [(qkT[0][:, i, row(s)], qkT[1][:, i, row(s)]) for i in range(KD)],
                                       [(cTp[0][:, s.odd, i, :], cTp[1][:, s.odd, i, :]) for i in range(KD)]).then_inc(s_full, 1)
                    if t is not None:
                        pe.wait_ge(pn_done, t.b + 1)
                        at_least(pe, pt_lo, t.b - 1)
                        for c in range(SC):
                            last = nc.tensor.transpose(k.ps[:C, 2 + t.odd, c * T:(c + 1) * T],
                                                       pr[:, t.odd, c * C:(c + 1) * C], k.ident[:T, :T])
                        last.then_inc(t_full, 1)
                    if m is not None:
                        pe.wait_ge(pt_lo, m.b + 1)
                        pe.wait_ge(cr_lo, m.b + 3)
                        pe.wait_ge(m_lo, m.b)
                        for i in range(KD):
                            last = three_products(nc, k.ps[:, 4 + m.odd, i * T:(i + 1) * T],
                                                  [(cRp[0][:, m.odd, c, i * P:(i + 1) * P], cRp[1][:, m.odd, c, i * P:(i + 1) * P])
                                                   for c in range(SC)],
                                                  [(pT[0][:, m.odd, c, :], pT[1][:, m.odd, c, :]) for c in range(SC)])
                        last.then_inc(m_full, 1)
                skewed(pe, emit)

            @block.scalar
            def _(act):
                def emit(s, t, m):
                    if s is not None:
                        act.wait_ge(c_in[s.odd], s.half * 32 + 32)
                        at_least(act, s_full, s.b - 1)
                        nc.scalar.activation(cTp[0][:, s.odd], cT[:, s.odd], ACT.Copy).then_inc(ct_hi, 1)
                        act.wait_ge(m_full, 3 + s.b - 1)
                        nc.scalar.activation(cRp[0][:, s.odd], cR[:, s.odd], ACT.Copy).then_inc(cr_hi, 1)
                        act.wait_ge(bias_step, 3 * s.b + 3)
                        at_least(act, t_full, s.b - 1)
                        nc.scalar.activation(pr[:, s.odd, :], k.ps[:T, s.odd, :S], ACT.Exp, bias=small_t[:, s.odd, 1:2],
                                             scale=SCALE, accum_out=small_t[:, s.odd, 2:3]).then_inc(p_done, 1)
                    if t is not None:
                        act.wait_ge(t_full, t.b + 1)
                        act.wait_ge(m_full, 3 + t.b - 1)
                        nc.scalar.activation(pT[0][:, t.odd], k.ps[:C, 2 + t.odd, 0:SC * T].rearrange("p (c q) -> p c q", c=SC),
                                             ACT.Copy).then_inc(pt_hi, 1)
                    if m is not None:
                        act.wait_ge(m_full, 3 + m.b + 1)
                        nc.scalar.activation(mT[0][:, :, row(m)], k.ps[:, 4 + m.odd, 0:KD * T].rearrange("p (c q) -> p c q", c=KD),
                                             ACT.Copy).then_inc(m_hi, 1)
                skewed(act, emit)

            @block.vector
            def _(dve):
                dve.sem_inc(ct_lo, 2)
                dve.sem_inc(m_lo, 1)

                def emit(s, t, m):
                    if s is not None:
                        dve.wait_ge(ct_hi, s.b + 1)
                        nc.vector.tensor_tensor(cTp[1][:, s.odd], cT[:, s.odd], cTp[0][:, s.odd], ALU.subtract).then_inc(ct_lo, 1)
                    if t is not None:
                        dve.wait_ge(p_done, t.b + 1)
                        nc.vector.reciprocal(small_t[:, t.odd, 3:4], small_t[:, t.odd, 2:3]).then_inc(pn_done_r, 1)
                        dve.wait_ge(pn_done_r, t.b + 1)
                        nc.vector.tensor_scalar(pr[:, t.odd, :], pr[:, t.odd, :], small_t[:, t.odd, 3:4], None,
                                                ALU.mult).then_inc(pn_done, 1)
                    if s is not None:
                        dve.wait_ge(s_full, s.b + 1)
                        at_least(dve, p_done, s.b - 1)
                        nc.vector.reduce_max(small_t[:, s.odd, 0:1], k.ps[:T, s.odd, :S], AX).then_inc(bias_step, 1)
                        dve.wait_ge(bias_step, 3 * s.b + 1)
                        nc.vector.tensor_tensor(small_t[:, s.odd, 0:1], small_t[:, s.odd, 0:1], one(qbk, s), ALU.add).then_inc(bias_step, 1)
                        dve.wait_ge(bias_step, 3 * s.b + 2)
                        nc.vector.scalar_tensor_tensor(small_t[:, s.odd, 1:2], one(qbk, s), small_t[:, s.odd, 0:1],
                                                       scale_t[:], ALU.subtract, ALU.mult).then_inc(bias_step, 1)
                    if t is not None:
                        dve.wait_ge(pt_hi, t.b + 1)
                        nc.vector.tensor_tensor(pT[1][:, t.odd], k.ps[:C, 2 + t.odd, 0:SC * T].rearrange("p (c q) -> p c q", c=SC),
                                                pT[0][:, t.odd], ALU.subtract).then_inc(pt_lo, 1)
                    if m is not None:
                        dve.wait_ge(m_hi, m.b + 1)
                        nc.vector.tensor_tensor(mT[1][:, :, row(m)], k.ps[:, 4 + m.odd, 0:KD * T].rearrange("p (c q) -> p c q", c=KD),
                                                mT[0][:, :, row(m)], ALU.subtract).then_inc(m_lo, 1)
                nc.vector.memset(scale_t[:], SCALE).then_inc(scale_set, 1)
                dve.wait_ge(scale_set, 1)
                skewed(dve, emit)

        tmp = sb("tmp", [P, 2, GT], F32)
        uT = [sb(f"uT{p}", [P, 2, KD, GT], BF16) for p in ("hi", "lo")]
        v_full, v_used, u_step, u_hi, u_lo, y_full, y_used, sum_done = (
            sem(s) for s in ("vfull", "vused", "ustep", "uhi", "ulo", "yfull", "yused", "sumdone"))
        with nc.Block() as block:
            @block.tensor
            def _(pe):
                def values(g):
                    for m in range(KD):
                        n = g * KD + m
                        if n >= 2:
                            pe.wait_ge(v_used, n - 1)
                        three_products(nc, k.ps[:, n % 2, :GT],
                                       [(wv[0][:, t, m * P:(m + 1) * P], wv[1][:, t, m * P:(m + 1) * P]) for t in range(KD)],
                                       [(mT[0][:, t, cols(g)], mT[1][:, t, cols(g)]) for t in range(KD)]).then_inc(v_full, 1)
                values(0)
                for g in range(NG):
                    if g + 1 < NG:
                        values(g + 1)
                    pe.wait_ge(u_lo, KD * (g + 1))
                    for i in range(GB):
                        n = GB * g + i
                        if n >= 4:
                            pe.wait_ge(y_used, n - 3)
                        three_products(nc, k.ps[:T, 4 + n % 4, :D],
                                       [(uT[0][:, g % 2, t, i * T:(i + 1) * T], uT[1][:, g % 2, t, i * T:(i + 1) * T])
                                        for t in range(KD)],
                                       [(wo[0][:, t, :], wo[1][:, t, :]) for t in range(KD)]).then_inc(y_full, 1)

            @block.vector
            def _(dve):
                def u(g):
                    for m in range(KD):
                        n = g * KD + m
                        dve.wait_ge(v_full, n + 1)
                        if n >= 2:
                            dve.wait_ge(u_lo, n - 1)
                        nc.vector.scalar_tensor_tensor(tmp[:, n % 2, :], k.ps[:, n % 2, :GT], bias[:, 2, m:m + 1],
                                                       k.xT[0][:, m, cols(g)], ALU.add, ALU.add).then_inc(v_used, 1)
                        dve.wait_ge(v_used, n + 1)
                        nc.vector.tensor_tensor(tmp[:, n % 2, :], tmp[:, n % 2, :], k.xT[1][:, m, cols(g)], ALU.add).then_inc(u_step, 1)
                        dve.wait_ge(u_step, n + 1)
                        if g >= 2:
                            dve.wait_ge(y_full, GB * (g - 1))
                        nc.vector.tensor_copy(uT[0][:, g % 2, m, :], tmp[:, n % 2, :]).then_inc(u_hi, 1)
                        dve.wait_ge(u_hi, n + 1)
                        nc.vector.tensor_tensor(uT[1][:, g % 2, m, :], tmp[:, n % 2, :], uT[0][:, g % 2, m, :],
                                                ALU.subtract).then_inc(u_lo, 1)
                u(0)
                for g in range(NG):
                    if g + 1 < NG:
                        u(g + 1)
                    for i in range(GB):
                        n = GB * g + i
                        dve.wait_ge(y_full, n + 1)
                        nc.vector.tensor_tensor(k.xs[:, n, :], k.ps[:T, 4 + n % 4, :D], k.xs[:, n, :], ALU.add).then_inc(y_used, 1)
                        dve.wait_ge(y_used, n + 1)
                        nc.vector.tensor_tensor(k.xs[:, n, :], k.xs[:, n, :], bo_b[:], ALU.add).then_inc(sum_done, 1)
                dve.wait_ge(sum_done, B)


def l1_experts(nc, k, a):
    with ExitStack() as ctx:
        sb = lambda name, shape, dt: k.sb("f1_" + name, shape, dt, ctx)
        sem = lambda name: k.sem("f1_" + name)
        mv2, rstd2 = sb("mv2", [T, B, 2], F32), sb("rstd2", [T, B], F32)
        normalise(nc, k, "n3", again=(mv2, rstd2))
        gate = sb("gate", [T, B, E1], F32)
        rn = sb("rn", [P, 2, KD], F32)
        ln = sb("ln", [P, 2, E1, HM], F32)
        on = sb("on", [T, 2, D], F32)
        raw1 = sb("raw1", [P, 2, KD, HID], F32)
        raw2 = sb("raw2", [P, 2, HM, D], F32)
        w1 = [sb(f"w1{p}", [P, E1, KD, HID], BF16) for p in ("hi", "lo")]
        w2 = [sb(f"w2{p}", [P, E1, HM, D], BF16) for p in ("hi", "lo")]
        w_in = [sem("win0"), sem("win1")]
        rn_in, vec_in, on_done, w1_hi, w1_lo, w2_hi, w2_lo = (
            sem(s) for s in ("rnin", "vecin", "on", "w1hi", "w1lo", "w2hi", "w2lo"))
        with nc.Block() as block:
            @block.sync
            def _(sp):
                for i, n in enumerate(("rn_g", "rn_b")):
                    sp.dma_start(rn[:, i, :], a["F1_" + n]).then_inc(rn_in, 16)
                for i, n in enumerate(("ln_g", "ln_b")):
                    sp.dma_start(ln[:, i], a["F1_" + n]).then_inc(vec_in, 16)
                for i, n in enumerate(("on_g", "on_b")):
                    sp.dma_start(on[:, i, :], a["F1_" + n].partition_broadcast(T)).then_inc(vec_in, 16)
                for e in range(E1):
                    if e >= 2:
                        sp.wait_ge(w1_lo, e - 1)
                        sp.wait_ge(w2_lo, e - 1)
                    sp.dma_start(raw1[:, e % 2], a["F1_w1"][e].rearrange("(t p) n -> p t n", p=P)).then_inc(w_in[e % 2], 16)
                    sp.dma_start(raw2[:, e % 2], a["F1_w2"][e].rearrange("(t p) n -> p t n", p=P)).then_inc(w_in[e % 2], 16)

            @block.scalar
            def _(act):
                for e in range(E1):
                    act.wait_ge(w_in[e % 2], 32 * (e // 2 + 1))
                    nc.scalar.activation(w1[0][:, e], raw1[:, e % 2], ACT.Copy).then_inc(w1_hi, 1)
                    nc.scalar.activation(w2[0][:, e], raw2[:, e % 2], ACT.Copy).then_inc(w2_hi, 1)

            @block.vector
            def _(dve):
                for e in range(E1):
                    dve.wait_ge(w1_hi, e + 1)
                    nc.vector.tensor_tensor(w1[1][:, e], raw1[:, e % 2], w1[0][:, e], ALU.subtract).then_inc(w1_lo, 1)
                    dve.wait_ge(w2_hi, e + 1)
                    nc.vector.tensor_tensor(w2[1][:, e], raw2[:, e % 2], w2[0][:, e], ALU.subtract).then_inc(w2_lo, 1)
                dve.wait_ge(vec_in, 64)
                nc.vector.tensor_scalar(on[:], on[:], k.tg_f[:T, 1:2], None, ALU.mult).then_inc(on_done, 1)
                dve.wait_ge(on_done, 1)
                dve.wait_ge(w2_lo, E1)
                dve.wait_ge(rn_in, 32)

        with ExitStack() as rctx:
            route(nc, k, "f1", a["F1_router_w"].rearrange("(t p) e -> p t e", p=P), E1, gate, L1_GATE_EPS,
                  1.0, rctx, affine=(rn[:, 0, :], rn[:, 1, :], mv2[:, :, 0], rstd2[:]))

        acc = sb("acc", [T, B, D], F32)
        stats, mv = sb("stats", [T, 2, 6], F32), sb("mv", [T, 2, 2], F32)
        std, rstd, shift, eps = (sb(n, [T, 2], F32) for n in ("std", "rstd", "shift", "eps"))
        z = sb("z", [T, 2, HID], F32)
        rf = sb("rf", [P, 2, HM, T], F32)
        rh, rl = sb("rh", [P, 2, HM, T], BF16), sb("rl", [P, 2, HM, T], BF16)
        (eps_set, up_full, st_done, var_done, std_done, rstd_done, shift_done, z_done, t_full, relu_done, r_hi, r_lo,
         y_full, y_used) = (sem(s) for s in ("epsset", "upfull", "st", "var", "std", "rstd", "shift", "z", "tfull",
                                             "relu", "rhi", "rlo", "yfull", "yused"))

        passed = sem("passed")

        class Unit:
            def __init__(self, e, r):
                self.e, self.r, self.b, self.odd, self.n = e, r, r.b, r.odd, e * B + r.b

        def units(eng, emit):
            for e in range(E1):
                PEEL = 2 if e else 4
                before = lambda r: Unit(e, turn(r)) if r >= 0 else Unit(e - 1, turn(B + r)) if e else None
                for r in range(PEEL):
                    emit(Unit(e, turn(r)), before(r - 1), before(r - 2))
                h = PEEL // 2
                with eng.Fori(0, (B - PEEL) // 2) as i:
                    at = lambda r: Unit(e, Turn(2 * (i + h) + r, i + h + r // 2, r % 2))
                    emit(at(0), at(-1), at(-2))
                    emit(at(1), at(0), at(-1))
            emit(None, Unit(E1 - 1, turn(B - 1)), Unit(E1 - 1, turn(B - 2)))
            emit(None, None, Unit(E1 - 1, turn(B - 1)))

        with nc.Block() as block:
            @block.tensor
            def _(pe):
                def emit(s, t, m):
                    if s is not None:
                        at_least(pe, z_done, s.n - 1)
                        three_products(nc, k.ps[:T, s.odd, :],
                                       [(k.xT[0][:, i, bass.ds(s.b * T, T)], k.xT[1][:, i, bass.ds(s.b * T, T)]) for i in range(KD)],
                                       [(w1[0][:, s.e, i, :], w1[1][:, s.e, i, :]) for i in range(KD)]).then_inc(up_full, 1)
                    if t is not None:
                        pe.wait_ge(z_done, t.n + 1)
                        at_least(pe, relu_done, HM * (t.n - 1))
                        for i in range(HM):
                            last = nc.tensor.transpose(k.ps[:, 2 + t.odd, i * T:(i + 1) * T], z[:, t.odd, i * P:(i + 1) * P],
                                                       k.ident[:T, :T])
                        last.then_inc(t_full, 1)
                    if m is not None:
                        pe.wait_ge(r_lo, m.n + 1)
                        pe.wait_ge(y_used, m.n)
                        three_products(nc, k.ps[:T, 4 + m.odd, :D],
                                       [(rh[:, m.odd, i, :], rl[:, m.odd, i, :]) for i in range(HM)],
                                       [(w2[0][:, m.e, i, :], w2[1][:, m.e, i, :]) for i in range(HM)]).then_inc(y_full, 1)
                units(pe, emit)

            @block.scalar
            def _(act):
                act.wait_ge(eps_set, 1)

                def emit(s, t, m):
                    if s is not None:
                        act.wait_ge(var_done, s.n + 1)
                        at_least(act, rstd_done, s.n - 1)
                        nc.scalar.activation(std[:, s.odd:s.odd + 1], mv[:, s.odd, 1:2], ACT.Sqrt, bias=eps[:, 0:1]).then_inc(std_done, 1)
                    if t is not None:
                        act.wait_ge(t_full, t.n + 1)
                        at_least(act, r_lo, t.n - 1)
                        for i in range(HM):
                            nc.scalar.activation(rf[:, t.odd, i, :], k.ps[:, 2 + t.odd, i * T:(i + 1) * T], ACT.Relu,
                                                 bias=ln[:, 1, t.e, i:i + 1], scale=ln[:, 0, t.e, i:i + 1]).then_inc(relu_done, 1)
                    if s is not None:
                        act.wait_ge(shift_done, s.n + 1)
                        at_least(act, t_full, s.n - 1)
                        nc.scalar.activation(z[:, s.odd, :], k.ps[:T, s.odd, :], ACT.Identity, bias=shift[:, s.odd:s.odd + 1],
                                             scale=rstd[:, s.odd:s.odd + 1]).then_inc(z_done, 1)
                units(act, emit)

            @block.gpsimd
            def _(pool):
                def emit(s, t, m):
                    if t is not None:
                        pool.wait_ge(r_hi, t.n + 1)
                        at_least(pool, y_full, t.n - 1)
                        nc.gpsimd.tensor_tensor(rl[:, t.odd], rf[:, t.odd], rh[:, t.odd], ALU.subtract).then_inc(r_lo, 1)
                units(pool, emit)

            @block.vector
            def _(dve):
                dve.sem_inc(y_used, 1)
                nc.vector.memset(eps[:], LN_EPS).then_inc(eps_set, 1)
                dve.wait_ge(eps_set, 1)

                def emit(s, t, m):
                    if s is not None:
                        dve.wait_ge(up_full, s.n + 1)
                        nc.vector.bn_stats(stats[:, s.odd, :], k.ps[:T, s.odd, :]).then_inc(st_done, 1)
                        at_least(dve, std_done, s.n - 1)
                        dve.wait_ge(st_done, s.n + 1)
                        dve.sem_inc(passed, 1)
                        nc.vector.bn_aggr(mv[:, s.odd, :], stats[:, s.odd, :]).then_inc(var_done, 1)
                        dve.wait_ge(std_done, s.n + 1)
                        at_least(dve, z_done, s.n - 1)
                        nc.vector.reciprocal(rstd[:, s.odd:s.odd + 1], std[:, s.odd:s.odd + 1]).then_inc(rstd_done, 1)
                        dve.wait_ge(rstd_done, s.n + 1)
                        nc.vector.scalar_tensor_tensor(shift[:, s.odd:s.odd + 1], mv[:, s.odd, 0:1], -1.0, rstd[:, s.odd:s.odd + 1],
                                                       ALU.mult, ALU.mult).then_inc(shift_done, 1)
                    if t is not None:
                        dve.wait_ge(relu_done, HM * t.n + HM)
                        at_least(dve, y_full, t.n - 1)
                        nc.vector.tensor_copy(rh[:, t.odd], rf[:, t.odd]).then_inc(r_hi, 1)
                    if m is not None:
                        dve.wait_ge(y_full, m.n + 1)
                        y, o, g = k.ps[:T, 4 + m.odd, :D], acc[:, bass.ds(m.b, 1), :].rearrange("p o d -> p (o d)"), gate[:, bass.ds(m.b, 1), m.e]
                        if m.e == 0:
                            nc.vector.tensor_scalar(o, y, g, None, ALU.mult).then_inc(y_used, 1)
                        else:
                            dve.wait_ge(y_used, m.n - B + 2)
                            nc.vector.scalar_tensor_tensor(o, y, g, o, ALU.mult, ALU.add).then_inc(y_used, 1)
                units(dve, emit)

        s_all, stats_all = sb("sall", [T, B], F32), sb("statsall", [T, B, 6], F32)
        a_done, v_done, sq_done, r_done, n_done, g_done, add_done, x_done, stored = (
            sem(s) for s in ("ostat", "ovar", "osq", "or", "on1", "on2", "on3", "ox", "stored"))
        with nc.Block() as block:
            @block.vector
            def _(dve):
                for b in range(B):
                    nc.vector.bn_stats(stats_all[:, b, :], acc[:, b, :]).then_inc(a_done, 1)
                for b in range(B):
                    dve.wait_ge(a_done, b + 1)
                    nc.vector.bn_aggr(k.mv[:, b, :], stats_all[:, b, :]).then_inc(v_done, 1)
                dve.wait_ge(sq_done, 1)
                nc.vector.reciprocal(k.rstd[:], s_all[:]).then_inc(r_done, 1)
                dve.wait_ge(r_done, 1)
                for b in range(B):
                    nc.vector.tensor_scalar(acc[:, b, :], acc[:, b, :], k.mv[:, b, 0:1], k.rstd[:, b:b + 1],
                                            ALU.subtract, ALU.mult).then_inc(n_done, 1)
                for g in range(NG):
                    r = slice(GB * g, GB * (g + 1))
                    wide = lambda i: on[:, i, :].unsqueeze(1).broadcast_to([T, GB, D])
                    dve.wait_ge(n_done, GB * (g + 1))
                    nc.vector.tensor_tensor(acc[:, r, :], acc[:, r, :], wide(0), ALU.mult).then_inc(g_done, 1)
                    nc.vector.tensor_tensor(k.xs[:, r, :], k.xs[:, r, :], wide(1), ALU.add).then_inc(add_done, 1)
                    dve.wait_ge(g_done, g + 1)
                    dve.wait_ge(add_done, g + 1)
                    nc.vector.tensor_tensor(k.xs[:, r, :], k.xs[:, r, :], acc[:, r, :], ALU.add).then_inc(x_done, 1)

            @block.scalar
            def _(act):
                act.wait_ge(v_done, B)
                nc.scalar.activation(s_all[:], k.mv[:, :, 1], ACT.Sqrt, bias=eps[:, 0:1]).then_inc(sq_done, 1)

            @block.sync
            def _(sp):
                for g in range(NG):
                    sp.wait_ge(x_done, g + 1)
                    sp.dma_start(a["out"][GB * g:GB * (g + 1)].rearrange("b t d -> t b d"),
                                 k.xs[:, GB * g:GB * (g + 1), :]).then_inc(stored, 16)
                sp.wait_ge(stored, 16 * NG)


def store(nc, k, out):
    stored = k.sem("stored")
    with nc.Block() as block:
        @block.sync
        def _(sp):
            sp.dma_start(out.rearrange("b t d -> t b d"), k.xs[:]).then_inc(stored, 16)
            sp.wait_ge(stored, 16)


def build(nc, a, out, stages=4):
    a = dict(a, out=out)
    with ExitStack() as ctx:
        k = Core(nc, ctx)
        setup(nc, k, a["x"], a["g_xattn"], a["g_ffn"])
        normalise(nc, k, "n0")
        l0_attention(nc, k, a["ctxT"], a["L0_Wq"], a["L0_bq"], a["L0_Wk"], a["L0_bk"], a["L0_Wv"], a["L0_bv"],
                     a["L0_Wo"], a["L0_bo"])
        k.release()
        if stages >= 2:
            l0_experts(nc, k, a)
            k.release()
        if stages >= 3:
            l1_attention(nc, k, a)
            k.release()
        if stages >= 4:
            l1_experts(nc, k, a)
        else:
            store(nc, k, out)


def kernel(**inputs):
    import numpy as np
    import concourse.bacc as bacc
    from concourse import mybir as m
    from concourse.bass_utils import run_bass_kernel_spmd

    keep = np.ascontiguousarray
    by_feature = lambda v: keep(np.reshape(v, (KD, P)).T)
    of = {n: np.asarray(v) for n, v in inputs.items()}
    a = {"x": of["x"], "ctx": of["ctx_1024"], "ctxT": np.transpose(of["ctx_1024"], (0, 2, 1)),
         "g_xattn": of["g_xattn"], "g_ffn": of["g_ffn"], "L1_Wk": of["L1_xattn_Wk"]}
    for n in ("Wq", "Wk", "Wv"):
        a["L0_" + n] = np.reshape(np.transpose(of["L0_xattn_" + n], (1, 0, 2)), (D, D))
    a["L0_Wo"] = of["L0_xattn_Wo"]
    for n in ("Wq", "Wv", "Wo"):
        a["L1_" + n] = of["L1_xattn_" + n].T
    for layer in ("L0", "L1"):
        for n in ("bq", "bk", "bv"):
            a[f"{layer}_{n}"] = by_feature(of[f"{layer}_xattn_{n}"])
        a[f"{layer}_bo"] = of[f"{layer}_xattn_bo"]
    for n in ("router_w", "w1", "w2", "w1_s", "w2_s"):
        a["F0_" + n] = of["L0_ffn_" + n]
    for n in ("rms_w", "rms_w_s"):
        v = of["L0_ffn_" + n]
        a["F0_" + n] = np.transpose(np.reshape(v, (v.shape[0], KD, P)), (2, 0, 1))
    for n in ("w1", "w2", "on_g", "on_b"):
        a["F1_" + n] = of["L1_ffn_" + n]
    a["F1_router_w"] = of["L1_ffn_router_w"].T
    for n in ("rn_g", "rn_b"):
        a["F1_" + n] = by_feature(of["L1_ffn_" + n])
    for n in ("ln_g", "ln_b"):
        a["F1_" + n] = np.transpose(np.reshape(of["L1_ffn_" + n], (E1, HM, P)), (2, 0, 1))
    a = {n: keep(v) for n, v in a.items()}

    nc = bacc.Bacc("TRN2", target_bir_lowering=False, num_devices=1)
    args = {n: nc.dram_tensor(n, v.shape, m.dt.from_np(v.dtype), kind="ExternalInput").ap() for n, v in a.items()}
    out = nc.dram_tensor("out", (B, T, D), m.dt.float32, kind="ExternalOutput").ap()
    build(nc, args, out)
    return run_bass_kernel_spmd(nc, [a], core_ids=[0]).results[0]["out"]
```

```python
from contextlib import ExitStack

import concourse.bass as bass
from concourse import mybir

ALU = mybir.AluOpType
ACT = mybir.ActivationFunctionType
AX = mybir.AxisListType.X
F32 = mybir.dt.float32
BF16 = mybir.dt.bfloat16
U32 = mybir.dt.uint32

P = 128
B, T, D = 16, 112, 256
S, SC, C = 375, 3, 125
KD = D // P
H, DH = 16, 16
N = B * T
GB = 4
NG = B // GB
GT = GB * T
HID = 512
HM = HID // P
E0, E0S, E1 = 14, 2, 4
QW = 2 * T
LN_EPS = 1e-5
RMS_EPS = 1.1920929e-07
L0_GATE_EPS, L1_GATE_EPS = 1e-9, 1e-8


def at_least(engine, sem, value):
    if isinstance(value, int) and value <= 0:
        return
    engine.wait_ge(sem, value)


def three_products(nc, out, left, right, first=True, last=True):
    steps = []
    for (lh, ll), (rh, rl) in zip(left, right):
        steps += [(lh, rh), (ll, rh), (lh, rl)]
    for i, (l, r) in enumerate(steps):
        ins = nc.tensor.matmul(out, l, r, start=first and i == 0, stop=last and i == len(steps) - 1)
    return ins


class Core:

    def __init__(self, nc, ctx):
        self.nc, self.ctx = nc, ctx
        self.sems = []
        self.xs = self.sb("xs", [T, B, D], F32)
        self.xn = self.sb("xn", [T, B, D], F32)
        self.xT = [self.sb(f"xT_{p}", [P, KD, N], BF16) for p in ("hi", "lo")]
        self.ident = self.sb("ident", [P, P], F32)
        self.g_x = self.sb("g_x", [P, 2], F32)
        self.g_f = self.sb("g_f", [P, 2], F32)
        self.tg_x = self.sb("tg_x", [P, 2], F32)
        self.tg_f = self.sb("tg_f", [P, 2], F32)
        self.mv = self.sb("mv", [T, B, 2], F32)
        self.rstd = self.sb("rstd", [T, B], F32)
        self.ps = ctx.enter_context(nc.psum_tensor("ps", [P, 8, 512], F32))

    def sb(self, name, shape, dt, ctx=None):
        return (ctx or self.ctx).enter_context(self.nc.sbuf_tensor(name, shape, dt))

    def sem(self, name):
        self.sems.append(self.nc.alloc_semaphore(name=name))
        return self.sems[-1]

    def release(self):
        self.nc.all_engine_barrier()
        self.nc.clear_and_free_semaphores(self.sems)
        self.nc.all_engine_barrier()
        self.sems = []


def setup(nc, k, x, g_xattn, g_ffn):
    x_in, g_in, id_zero, id_done, tanh_done = (k.sem("setup_" + s) for s in
                                               ("x_in", "g_in", "id_zero", "id_done", "tanh"))
    with nc.Block() as block:
        @block.sync
        def _(sp):
            sp.dma_start(k.xs[:], x.rearrange("b t d -> t b d")).then_inc(x_in, 16)
            sp.dma_start(k.g_x[:], g_xattn.partition_broadcast(P)).then_inc(g_in, 16)
            sp.dma_start(k.g_f[:], g_ffn.partition_broadcast(P)).then_inc(g_in, 16)
            sp.wait_ge(x_in, 16)

        @block.gpsimd
        def _(pool):
            nc.gpsimd.memset(k.ident[:], 0.0).then_inc(id_zero, 1)
            pool.wait_ge(id_zero, 1)
            nc.gpsimd.affine_select(out=k.ident[:], in_=k.ident[:], compare_op=ALU.not_equal, fill=1.0,
                                    base=0, pattern=[[-1, P]], channel_multiplier=1).then_inc(id_done, 1)
            pool.wait_ge(id_done, 1)

        @block.scalar
        def _(act):
            act.wait_ge(g_in, 32)
            nc.scalar.activation(k.tg_x[:], k.g_x[:], ACT.Tanh).then_inc(tanh_done, 1)
            nc.scalar.activation(k.tg_f[:], k.g_f[:], ACT.Tanh).then_inc(tanh_done, 1)
            act.wait_ge(tanh_done, 2)


def normalise(nc, k, name, rms=None, again=None):
    stats_done, var_done, root_done, rstd_done, xn_done, full, hi_done, lo_done, sq_done, sq_root, r_done, aux = (
        k.sem(f"{name}_{s}") for s in ("stats", "var", "root", "rstd", "xn", "full", "hi", "lo", "sq",
                                       "sqroot", "r", "aux"))
    with ExitStack() as ctx:
        stats = k.sb(f"{name}_stats", [T, B, 6], F32, ctx)
        root = k.sb(f"{name}_root", [T, B], F32, ctx)
        sums = k.sb(f"{name}_sums", [T, B], F32, ctx)
        sq = k.sb(f"{name}_sq", [T, 2, D], F32, ctx)
        eps = k.sb(f"{name}_eps", [T, 2], F32, ctx)
        eps_set = k.sem(f"{name}_epsset")
        with nc.Block() as block:
            @block.vector
            def _(dve):
                nc.vector.memset(eps[:, 0:1], LN_EPS).then_inc(eps_set, 1)
                nc.vector.memset(eps[:, 1:2], RMS_EPS).then_inc(eps_set, 1)
                for b in range(B):
                    nc.vector.bn_stats(stats[:, b, :], k.xs[:, b, :]).then_inc(stats_done, 1)
                for b in range(B):
                    dve.wait_ge(stats_done, b + 1)
                    nc.vector.bn_aggr(k.mv[:, b, :], stats[:, b, :]).then_inc(var_done, 1)
                dve.wait_ge(root_done, 1)
                nc.vector.reciprocal(k.rstd[:], root[:]).then_inc(rstd_done, 1)
                dve.wait_ge(rstd_done, 1)
                for b in range(B):
                    nc.vector.tensor_scalar(k.xn[:, b, :], k.xs[:, b, :], k.mv[:, b, 0:1], k.rstd[:, b:b + 1],
                                            ALU.subtract, ALU.mult).then_inc(xn_done, 1)
                if rms:
                    dve.wait_ge(sq_root, 1)
                    nc.vector.reciprocal(rms[0][:], rms[1][:]).then_inc(r_done, 1)
                    dve.wait_ge(r_done, 1)
                    for b in range(B):
                        nc.vector.tensor_scalar(k.xn[:, b, :], k.xn[:, b, :], rms[0][:, b:b + 1], None,
                                                ALU.mult).then_inc(xn_done, 1)
                if again:
                    for b in range(B):
                        dve.wait_ge(xn_done, b + 1)
                        nc.vector.bn_stats(stats[:, b, :], k.xn[:, b, :]).then_inc(stats_done, 1)
                    for b in range(B):
                        dve.wait_ge(stats_done, B + b + 1)
                        nc.vector.bn_aggr(again[0][:, b, :], stats[:, b, :]).then_inc(aux, 1)
                    dve.wait_ge(sq_root, 1)
                    nc.vector.reciprocal(again[1][:], root[:]).then_inc(r_done, 1)
                for g in range(NG):
                    dve.wait_ge(hi_done, g + 1)
                    bank = 2 * (g % 2)
                    nc.vector.tensor_tensor(k.xT[1][:, :, g * GT:(g + 1) * GT], k.ps[:, bank:bank + 2, :GT],
                                            k.xT[0][:, :, g * GT:(g + 1) * GT], ALU.subtract).then_inc(lo_done, 1)

            @block.scalar
            def _(act):
                act.wait_ge(var_done, B)
                act.wait_ge(eps_set, 2)
                nc.scalar.activation(root[:], k.mv[:, :, 1], ACT.Sqrt, bias=eps[:, 0:1]).then_inc(root_done, 1)
                if rms:
                    for b in range(B):
                        act.wait_ge(xn_done, b + 1)
                        if b >= 2:
                            act.wait_ge(sq_done, b - 1)
                        nc.scalar.activation(sq[:, b % 2, :], k.xn[:, b, :], ACT.Square,
                                             accum_out=sums[:, b:b + 1]).then_inc(sq_done, 1)
                    act.wait_ge(sq_done, B)
                    nc.scalar.activation(rms[1][:], sums[:], ACT.Sqrt, bias=eps[:, 1:2],
                                         scale=1.0 / D).then_inc(sq_root, 1)
                if again:
                    act.wait_ge(rstd_done, 1)
                    act.wait_ge(aux, B)
                    nc.scalar.activation(root[:], again[0][:, :, 1], ACT.Sqrt, bias=eps[:, 0:1]).then_inc(sq_root, 1)
                for g in range(NG):
                    act.wait_ge(full, g + 1)
                    bank = 2 * (g % 2)
                    nc.scalar.activation(k.xT[0][:, :, g * GT:(g + 1) * GT], k.ps[:, bank:bank + 2, :GT],
                                         ACT.Copy).then_inc(hi_done, 1)

            @block.tensor
            def _(pe):
                for g in range(NG):
                    pe.wait_ge(xn_done, (B if rms else 0) + GB * (g + 1))
                    if g >= 2:
                        pe.wait_ge(lo_done, g - 1)
                    bank = 2 * (g % 2)
                    for i in range(GB):
                        for t in range(KD):
                            last = nc.tensor.transpose(k.ps[:, bank + t, i * T:(i + 1) * T],
                                                       k.xn[:, GB * g + i, t * P:(t + 1) * P], k.ident[:T, :T])
                    last.then_inc(full, 1)


def load_square(nc, k, name, weights, scales, ctx):
    n = len(weights)
    parts = [[k.sb(f"{name}_w{i}_{p}", [P, KD, D], BF16, ctx) for p in ("hi", "lo")] for i in range(n)]
    staging = ExitStack()
    raw = k.sb(f"{name}_raw", [P, n, KD, D], F32, staging)
    w_in = [k.sem(f"{name}_in{i}") for i in range(n)]
    scaled, hi_done, lo_done = (k.sem(f"{name}_{s}") for s in ("scaled", "whi", "wlo"))
    with nc.Block() as block:
        @block.sync
        def _(sp):
            for i, w in enumerate(weights):
                sp.dma_start(raw[:, i], w.rearrange("(t p) n -> p t n", p=P)).then_inc(w_in[i], 16)

        @block.vector
        def _(dve):
            turned = 0
            for i in range(n):
                dve.wait_ge(w_in[i], 16)
                if scales[i] is not None:
                    nc.vector.tensor_scalar(raw[:, i], raw[:, i], scales[i], None, ALU.mult).then_inc(scaled, 1)
                    turned += 1
                    dve.wait_ge(scaled, turned)
                nc.vector.tensor_copy(parts[i][0][:], raw[:, i]).then_inc(hi_done, 1)
                dve.wait_ge(hi_done, i + 1)
                nc.vector.tensor_tensor(parts[i][1][:], raw[:, i], parts[i][0][:], ALU.subtract).then_inc(lo_done, 1)
            dve.wait_ge(lo_done, n)
    staging.close()
    return parts


class Turn:

    def __init__(self, b, half, odd):
        self.b, self.half, self.odd = b, half, odd


def turn(b):
    return Turn(b, b // 2, b % 2)


class Ring(Turn):

    def __init__(self, quarter, slot):
        super().__init__(4 * quarter + slot, 2 * quarter + slot // 2, slot % 2)
        self.quarter, self.slot = quarter, slot


def ring(b):
    return Ring(b // 4, b % 4)


def l0_attention(nc, k, ctxT, Wq, bq, Wk, bk, Wv, bv, Wo, bo):
    with ExitStack() as ctx:
        sb = lambda name, shape, dt: k.sb("a0_" + name, shape, dt, ctx)
        sem = lambda name: k.sem("a0_" + name)
        wq, wk, wv, wo = load_square(nc, k, "a0", [Wq, Wk, Wv, Wo], [None, None, None, k.tg_x[:, 0:1]], ctx)
        bias = sb("bias", [P, 3, KD], F32)
        bo_b = sb("bo", [T, D], F32)
        pair = sb("pair", [P, 2], F32)
        JJ = P // (2 * DH)
        NJ = KD * JJ
        stkQ = sb("stkQ", [98, B, KD, JJ, QW], BF16)
        early = ExitStack()
        qf = k.sb("a0_qf", [P, KD, N], F32, early)
        QS = k.sb("a0_QS", [P, 2, B, KD, 2, T], BF16, early)
        b_in, bo_in, pair_sum, pair_done, q_full, q_copied, bo_scaled, q_hi, q_lo, q_in = (
            sem(s) for s in ("b_in", "bo_in", "pairsum", "pair", "qfull", "qcopied", "boscaled", "qhi", "qlo", "qin"))

        with nc.Block() as block:
            @block.sync
            def _(sp):
                for i, v in enumerate((bq, bk, bv)):
                    sp.dma_start(bias[:, i, :], v).then_inc(b_in, 16)
                sp.dma_start(bo_b[:], bo.partition_broadcast(T)).then_inc(bo_in, 16)
                for g in range(NG):
                    rows = slice(GB * g, GB * (g + 1))
                    sp.wait_ge(q_lo, (g + 1) * KD * 2)
                    for jj in range(JJ):
                        for a, part in ((0, 0), (1, 0), (2, 1)):
                            sp.dma_start(stkQ[32 * a:32 * a + 32, rows, :, jj, :],
                                         QS[32 * jj:32 * jj + 32, part, rows].rearrange("p b t h q -> p b t (h q)")).then_inc(q_in, 16)
                sp.wait_ge(q_in, NG * 3 * JJ * 16)

            @block.vector
            def _(dve):
                nc.vector.tensor_reduce(pair[:], k.ident[:].rearrange("p (h two d) -> p two h d", two=2, d=DH),
                                        mybir.AxisListType.XY, ALU.add).then_inc(pair_sum, 1)
                dve.wait_ge(pair_sum, 1)
                nc.vector.tensor_scalar(pair[:], pair[:], DH ** -0.5, None, ALU.mult).then_inc(pair_done, 1)
                dve.wait_ge(bo_in, 16)
                nc.vector.tensor_scalar(bo_b[:], bo_b[:], k.tg_x[:T, 0:1], None, ALU.mult).then_inc(bo_scaled, 1)
                dve.wait_ge(bo_scaled, 1)
                dve.wait_ge(pair_done, 1)
                for g in range(NG):
                    rows = slice(GB * g, GB * (g + 1))
                    dve.wait_ge(q_copied, KD * (g + 1))
                    for t in range(KD):
                        q = qf[:, t, g * GT:(g + 1) * GT].rearrange("p (b q) -> p b q", q=T)
                        for h in range(2):
                            n = (g * KD + t) * 2 + h
                            nc.vector.tensor_scalar(QS[:, 0, rows, t, h, :], q, pair[:, h:h + 1], None, ALU.mult).then_inc(q_hi, 1)
                            dve.wait_ge(q_hi, n + 1)
                            nc.vector.scalar_tensor_tensor(QS[:, 1, rows, t, h, :], q, pair[:, h:h + 1],
                                                           QS[:, 0, rows, t, h, :], ALU.mult, ALU.subtract).then_inc(q_lo, 1)

            @block.tensor
            def _(pe):
                for g in range(NG):
                    for m in range(KD):
                        n = KD * g + m
                        if n >= 2:
                            pe.wait_ge(q_copied, n - 1)
                        three_products(nc, k.ps[:, n % 2, :GT],
                                       [(wq[0][:, t, m * P:(m + 1) * P], wq[1][:, t, m * P:(m + 1) * P]) for t in range(KD)],
                                       [(k.xT[0][:, t, g * GT:(g + 1) * GT], k.xT[1][:, t, g * GT:(g + 1) * GT])
                                        for t in range(KD)]).then_inc(q_full, 1)

            @block.scalar
            def _(act):
                act.wait_ge(b_in, 48)
                for g in range(NG):
                    for m in range(KD):
                        n = KD * g + m
                        act.wait_ge(q_full, n + 1)
                        nc.scalar.activation(qf[:, m, g * GT:(g + 1) * GT], k.ps[:, n % 2, :GT], ACT.Identity,
                                             bias=bias[:, 0, m:m + 1]).then_inc(q_copied, 1)
                act.wait_ge(q_copied, KD * NG)

        early.close()
        stkK = sb("stkK", [98, 4, KD, JJ, S], BF16)
        KS = sb("KS", [P, 2, 2, KD, S], BF16)
        ctxF = sb("ctxF", [P, 2, KD, S], F32)
        ctxH = sb("ctxH", [P, 2, KD, S], BF16)
        ctxL = sb("ctxL", [P, 2, KD, S], BF16)
        VW = 2 * DH + 1
        V = sb("V", [C, 4, SC, H, VW], BF16)
        PW = QW + 16
        PB, LAG = 4, 2
        Pf = sb("Pf", [C, PB, SC, QW], F32)
        Ph = sb("Ph", [C, PB, SC, PW], BF16)
        Pl = sb("Pl", [C, PB, SC, PW], BF16)
        mx = sb("mx", [T, 2, H], F32)
        cneg = sb("cneg", [H, 2, 2, T], BF16)
        rden = sb("rden", [T, 2, NJ], F32)
        osum = sb("osum", [T, 2, NJ, DH], F32)
        attn = k.xn
        psST = k.ps[:, 0:4, :].rearrange("p (u two) n -> p u (two n)", u=2)
        psMX = k.ps[:, 4:6, :]
        psPV = k.ps[:, 6, 0:NJ * VW].rearrange("p (h w) -> p h w", w=VW)
        psP = k.ps[:, 7, :]

        ones_set, passed, hi_by_act = sem("ones"), sem("passed"), sem("hibyact")
        ctx_in = [sem(f"ctxin{i}") for i in range(2)]
        k_in = [sem(f"kin{i}") for i in range(4)]
        c_in = [sem(f"cin{i}") for i in range(2)]
        (ctx_hi, ctx_lo, proj_full, part_hi, proj_free, turn_full, turn_free, st_full, exp_done, p_hi, p_lo, pv_full,
         mx_full, mx_red, c_hi, rden_done, pv_free, attn_done) = (sem(s) for s in (
             "ctxhi", "ctxlo", "projfull", "parthi", "projfree", "turnfull", "turnfree", "stfull", "expdone", "phi",
             "plo", "pvfull", "mxfull", "mxred", "chi", "rden", "pvfree", "attn"))
        K_IN = 3 * JJ * 16
        TASKS = 4
        HI_BY_ACT = (1, 4, 7)
        HI_BY_DVE = [j for j in range(NJ) if j not in HI_BY_ACT]

        def hi_before(j):
            return sum(i < j for i in HI_BY_DVE)

        def run(eng, emit):
            emit(None, None, None, (ring(0),), (ring(0), ring(1)))
            emit(None, None, ring(0), (ring(1),), (ring(2),))
            emit(None, ring(0), ring(1), (ring(2),), (ring(3),))
            for b in range(3):
                emit(ring(b), ring(b + 1), ring(b + 2), (ring(b + 3),), (ring(b + 4),))
            with eng.Fori(0, 2) as i:
                for u in range(3, 7):
                    at = lambda r: Ring(i + (u + r) // 4, (u + r) % 4)
                    emit(at(0), at(1), at(2), (at(3),), (at(4),))
            for b in range(11, B):
                at = lambda r: ring(b + r) if b + r < B else None
                some = lambda r: (at(r),) if at(r) else ()
                emit(at(0), at(1), at(2), some(3), some(4))

        psT = k.ps[:, 7, :]
        with nc.Block() as block:
            @block.sync
            def _(sp):
                def load(l):
                    if not isinstance(l.b, int) or l.b >= 2:
                        sp.wait_ge(ctx_lo, l.b - 1)
                    sp.sem_inc(passed, 1)
                    sp.dma_start(ctxF[:, l.odd], ctxT[bass.ds(l.b, 1)].rearrange("b (t p) s -> p (b t) s", p=P))\
                        .then_inc(ctx_in[l.odd], 16)

                def emit(b, n, w, x, l):
                    for row in l:
                        load(row)
                    if w is not None:
                        at_least(sp, st_full, w.b * NJ - 4 * NJ)
                        sp.wait_ge(proj_free, w.b * TASKS + 2)
                        for jj in range(JJ):
                            for a, part in ((0, 0), (1, 1), (2, 0)):
                                sp.dma_start(stkK[32 * a:32 * a + 32, w.slot, :, jj, :], KS[32 * jj:32 * jj + 32, w.odd, part])\
                                    .then_inc(k_in[w.slot], 16)
                    if n is not None:
                        sp.wait_ge(turn_free, n.b + 1)
                        for part in range(2):
                            sp.dma_start(stkQ[96 + part:97 + part, bass.ds(n.b, 1)].rearrange("o b t j (h q) -> o (b t j h) q", q=T),
                                         cneg[:, n.odd, part, :]).then_inc(c_in[n.odd], 16)
                run(sp, emit)

            @block.tensor
            def _(pe):
                def scores(b, j):
                    if j == 0:
                        pe.wait_ge(c_in[b.odd], b.half * 32 + 32)
                    at_least(pe, exp_done, b.b * NJ + (j - 1))
                    for c in range(SC):
                        last = nc.tensor.matmul(psST[:C, j % 2, c * 256:c * 256 + QW],
                                                stkK[:, b.slot, j // JJ, j % JJ, c * C:(c + 1) * C],
                                                stkQ[:, bass.ds(b.b, 1), j // JJ, j % JJ, :].rearrange("p o q -> p (o q)"),
                                                start=True, stop=True)
                    last.then_inc(st_full, 1)

                def values(b, j):
                    pe.wait_ge(p_lo, b.b * NJ + j + 1)
                    if j % JJ == 0:
                        at_least(pe, pv_free, b.b * 2 + j // JJ)
                    for h in range(2):
                        i = 0
                        for c in range(SC):
                            for part in (Ph, Pl):
                                last = nc.tensor.matmul(psPV[:, (2 * j + h) % NJ, :], part[:, j % PB, c, h * T:h * T + P],
                                                        V[:, b.slot, c, 2 * j + h, :], start=i == 0, stop=i == 2 * SC - 1)
                                i += 1
                    last.then_inc(pv_full, 1)

                def keys(w, m):
                    if m == 0:
                        pe.wait_ge(ctx_lo, w.b + 1)
                    at_least(pe, proj_free, w.b * TASKS + m)
                    if m == 0:
                        at_least(pe, turn_free, w.b - 1)
                    three_products(nc, psP[:, :S],
                                   [(wk[0][:, t, m * P:(m + 1) * P], wk[1][:, t, m * P:(m + 1) * P]) for t in range(KD)],
                                   [(ctxH[:, w.odd, t, :], ctxL[:, w.odd, t, :]) for t in range(KD)]).then_inc(proj_full, 1)

                def vals(w, i):
                    pe.wait_ge(proj_free, w.b * TASKS + 2 + i)
                    for c in ((0, 1), (2,))[i]:
                        last = three_products(nc, psP[:C, (c % 2) * D:(c % 2 + 1) * D],
                                              [(ctxH[:, w.odd, t, c * C:(c + 1) * C], ctxL[:, w.odd, t, c * C:(c + 1) * C])
                                               for t in range(KD)],
                                              [(wv[0][:, t, :], wv[1][:, t, :]) for t in range(KD)])
                    last.then_inc(proj_full, 1)

                def maxima(n, j):
                    if j == 0:
                        pe.wait_ge(k_in[n.slot], n.quarter * K_IN + K_IN)
                    at_least(pe, mx_red, n.b * NJ + j)
                    for h in range(2):
                        last = nc.tensor.matmul(psMX[:T, h, :S],
                                                stkQ[0:96, bass.ds(n.b, 1), j // JJ, j % JJ, h * T:(h + 1) * T].rearrange("p o q -> p (o q)"),
                                                stkK[0:96, n.slot, j // JJ, j % JJ, :], start=True, stop=True)
                    last.then_inc(mx_full, 1)

                def turn_maxima(n, w):
                    pe.wait_ge(mx_red, n.b * NJ + NJ)
                    if w is not None:
                        pe.wait_ge(proj_free, w.b * TASKS + TASKS)
                    nc.tensor.transpose(psT[:H, :T], mx[:, n.odd, :], k.ident[:T, :T]).then_inc(turn_full, 1)

                pe.wait_ge(ones_set, 5)

                def emit(b, n, w, x, l):
                    for s in range(NJ + LAG):
                        if n is not None and s < NJ:
                            maxima(n, s)
                        if w is not None and s < 4:
                            (keys if s < 2 else vals)(w, s % 2)
                        if b is not None and s < NJ:
                            scores(b, s)
                        if n is not None and s == NJ:
                            turn_maxima(n, w)
                        if b is not None and s >= LAG:
                            values(b, s - LAG)

                run(pe, emit)

            @block.scalar
            def _(act):
                def emit(b, n, w, x, l):
                    for s in range(NJ):
                        if w is not None and s < 4:
                            i = s
                            act.wait_ge(proj_full, w.b * TASKS + i + 1)
                            if i < 2:
                                if i == 0 and not (isinstance(w.b, int) and w.b < 2):
                                    act.wait_ge(k_in[(w.slot + 2) % 4], (w.quarter + (w.slot + 2) // 4) * K_IN)
                                nc.scalar.activation(KS[:, w.odd, 0, i, :], psP[:, :S], ACT.Identity,
                                                     bias=bias[:, 1, i:i + 1]).then_inc(part_hi, 1)
                            else:
                                if i == 2:
                                    at_least(act, pv_full, w.b * NJ - 4 * NJ + NJ)
                                c0, nc_ = ((0, 2), (2, 1))[i - 2]
                                nc.scalar.activation(V[:, w.slot, c0:c0 + nc_, :, 0:DH],
                                                     psP[:C, 0:nc_ * D].rearrange("p (c h d) -> p c h d", c=nc_, d=DH),
                                                     ACT.Copy).then_inc(part_hi, 1)
                        if b is not None:
                            act.wait_ge(st_full, b.b * NJ + s + 1)
                            scores = psST[:C, s % 2, 0:SC * 256].rearrange("p (c n) -> p c n", c=SC)[:, :, :QW]
                            if s in HI_BY_ACT:
                                at_least(act, pv_full, b.b * NJ + s + 1 - PB)
                                nc.scalar.activation(Ph[:, s % PB, :, :QW], scores, ACT.Exp).then_inc(hi_by_act, 1)
                            at_least(act, p_lo, b.b * NJ + s + 1 - PB)
                            nc.scalar.activation(Pf[:, s % PB], scores, ACT.Exp).then_inc(exp_done, 1)
                    for row in x:
                        act.wait_ge(ctx_in[row.odd], row.half * 16 + 16)
                        at_least(act, proj_full, row.b * TASKS - 2 * TASKS + TASKS)
                        nc.scalar.activation(ctxH[:, row.odd], ctxF[:, row.odd], ACT.Copy).then_inc(ctx_hi, 1)
                act.wait_ge(ones_set, 5)
                run(act, emit)

            @block.gpsimd
            def _(pool):
                nc.gpsimd.memset(Pl[:], 0.0).then_inc(ones_set, 1)
                pool.wait_ge(ones_set, 1)

                def emit(b, n, w, x, l):
                    for s in range(NJ):
                        if b is not None:
                            pool.wait_ge(exp_done, b.b * NJ + s + 1)
                            if s not in HI_BY_ACT:
                                pool.wait_ge(p_hi, b.b * len(HI_BY_DVE) + hi_before(s) + 1)
                            at_least(pool, pv_full, b.b * NJ + s + 1 - PB)
                            nc.gpsimd.tensor_tensor(Pl[:, s % PB, :, :QW], Pf[:, s % PB], Ph[:, s % PB, :, :QW],
                                                    ALU.subtract).then_inc(p_lo, 1)
                    for row in x:
                        pool.wait_ge(ctx_hi, row.b + 1)
                        nc.gpsimd.tensor_tensor(ctxL[:, row.odd], ctxF[:, row.odd], ctxH[:, row.odd], ALU.subtract).then_inc(ctx_lo, 1)
                run(pool, emit)

            @block.vector
            def _(dve):
                nc.vector.memset(Ph[:], 0.0).then_inc(ones_set, 1)
                nc.vector.memset(V[:], 1.0).then_inc(ones_set, 1)
                nc.vector.memset(stkK[96:98], 1.0).then_inc(ones_set, 1)
                nc.vector.memset(mx[:], 0.0).then_inc(ones_set, 1)
                dve.wait_ge(ones_set, 5)

                def reduce(n, j):
                    if j == 0:
                        at_least(dve, turn_full, n.b - 1)
                    dve.wait_ge(mx_full, n.b * NJ + j + 1)
                    nc.vector.reduce_max(mx[:, n.odd, 2 * j:2 * j + 2], psMX[:T, :, :S], AX).then_inc(mx_red, 1)

                def minus_maxima(n):
                    at_least(dve, c_in[n.odd], n.half * 32)
                    dve.wait_ge(turn_full, n.b + 1)
                    nc.vector.tensor_scalar(cneg[:, n.odd, 0, :], psT[:H, :T], -1.0, None, ALU.mult).then_inc(c_hi, 1)
                    dve.wait_ge(c_hi, n.b + 1)
                    nc.vector.scalar_tensor_tensor(cneg[:, n.odd, 1, :], psT[:H, :T], -1.0, cneg[:, n.odd, 0, :],
                                                   ALU.mult, ALU.subtract).then_inc(turn_free, 1)

                def finish(b, half):
                    dve.wait_ge(pv_full, b.b * NJ + JJ * (half + 1))
                    at_least(dve, attn_done, b.b * 2 + half - 1)
                    nc.vector.reciprocal(rden[:, half, :], psPV[:T, :, 2 * DH]).then_inc(rden_done, 1)
                    nc.vector.tensor_copy(osum[:, half], psPV[:T, :, 0:DH]).then_inc(rden_done, 1)
                    dve.wait_ge(rden_done, b.b * 4 + 2 * half + 2)
                    nc.vector.tensor_tensor(osum[:, half], psPV[:T, :, DH:2 * DH], osum[:, half],
                                            ALU.add).then_inc(pv_free, 1)
                    dve.wait_ge(pv_free, b.b * 2 + half + 1)
                    nc.vector.tensor_tensor(
                        attn[:, bass.ds(b.b, 1), half * P:(half + 1) * P].rearrange("p o (h d) -> p (o h) d", d=DH),
                        osum[:, half], rden[:, half, :].unsqueeze(2).broadcast_to([T, NJ, DH]), ALU.mult).then_inc(attn_done, 1)

                def emit(b, n, w, x, l):
                    for s in range(NJ):
                        if b is not None and s == 6:
                            finish(b, 0)
                        if n is not None:
                            reduce(n, s)
                        if w is not None and s < 4:
                            i = s
                            dve.wait_ge(part_hi, w.b * TASKS + i + 1)
                            if i < 2:
                                nc.vector.scalar_tensor_tensor(KS[:, w.odd, 1, i, :], psP[:, :S], bias[:, 1, i:i + 1],
                                                               KS[:, w.odd, 0, i, :], ALU.add, ALU.subtract).then_inc(proj_free, 1)
                            else:
                                c0, nc_ = ((0, 2), (2, 1))[i - 2]
                                nc.vector.tensor_tensor(V[:, w.slot, c0:c0 + nc_, :, DH:2 * DH],
                                                        psP[:C, 0:nc_ * D].rearrange("p (c h d) -> p c h d", c=nc_, d=DH),
                                                        V[:, w.slot, c0:c0 + nc_, :, 0:DH], ALU.subtract).then_inc(proj_free, 1)
                        if b is not None and s in HI_BY_DVE:
                            dve.wait_ge(exp_done, b.b * NJ + s + 1)
                            at_least(dve, pv_full, b.b * NJ + s + 1 - PB)
                            nc.vector.tensor_copy(Ph[:, s % PB, :, :QW], Pf[:, s % PB]).then_inc(p_hi, 1)
                    if n is not None:
                        minus_maxima(n)
                    if b is not None:
                        finish(b, 1)
                run(dve, emit)

        output_projection(nc, k, "a0", attn, bias[:, 2, :], wo, bo_b, ctx)


def output_projection(nc, k, name, attn, bv, wo, bo_b, ctx):
    aT = [k.sb(f"{name}_aT_{p}", [P, 2, KD, GT], BF16, ctx) for p in ("hi", "lo")]
    t_full, hi_done, lo_done, y_full, y_used, sum_done = (
        k.sem(f"{name}_o_{s}") for s in ("tfull", "hi", "lo", "yfull", "yused", "sum"))
    with nc.Block() as block:
        @block.tensor
        def _(pe):
            def turned(g):
                if g >= 2:
                    pe.wait_ge(lo_done, KD * (g - 1))
                for i in range(GB):
                    for t in range(KD):
                        last = nc.tensor.transpose(k.ps[:, 2 * (g % 2) + t, i * T:(i + 1) * T],
                                                   attn[:, GB * g + i, t * P:(t + 1) * P], k.ident[:T, :T])
                last.then_inc(t_full, 1)
            turned(0)
            for g in range(NG):
                if g + 1 < NG:
                    turned(g + 1)
                pe.wait_ge(lo_done, KD * (g + 1))
                for i in range(GB):
                    n = GB * g + i
                    if n >= 4:
                        pe.wait_ge(y_used, n - 3)
                    three_products(nc, k.ps[:T, 4 + n % 4, :D],
                                   [(aT[0][:, g % 2, t, i * T:(i + 1) * T], aT[1][:, g % 2, t, i * T:(i + 1) * T])
                                    for t in range(KD)],
                                   [(wo[0][:, t, :], wo[1][:, t, :]) for t in range(KD)]).then_inc(y_full, 1)

        @block.scalar
        def _(act):
            for g in range(NG):
                act.wait_ge(t_full, g + 1)
                if g >= 2:
                    act.wait_ge(y_full, GB * (g - 1))
                for t in range(KD):
                    nc.scalar.activation(aT[0][:, g % 2, t, :], k.ps[:, 2 * (g % 2) + t, :GT], ACT.Identity,
                                         bias=bv[:, t:t + 1]).then_inc(hi_done, 1)

        @block.vector
        def _(dve):
            def low(g):
                for t in range(KD):
                    dve.wait_ge(hi_done, KD * g + t + 1)
                    nc.vector.scalar_tensor_tensor(aT[1][:, g % 2, t, :], k.ps[:, 2 * (g % 2) + t, :GT], bv[:, t:t + 1],
                                                   aT[0][:, g % 2, t, :], ALU.add, ALU.subtract).then_inc(lo_done, 1)
            low(0)
            for g in range(NG):
                if g + 1 < NG:
                    low(g + 1)
                for i in range(GB):
                    n = GB * g + i
                    dve.wait_ge(y_full, n + 1)
                    nc.vector.tensor_tensor(k.xs[:, n, :], k.ps[:T, 4 + n % 4, :D], k.xs[:, n, :],
                                            ALU.add).then_inc(y_used, 1)
                    dve.wait_ge(y_used, n + 1)
                    nc.vector.tensor_tensor(k.xs[:, n, :], k.xs[:, n, :], bo_b[:], ALU.add).then_inc(sum_done, 1)
            dve.wait_ge(sum_done, B)




def linker(engine, sem):
    count = [0]

    def link(ins):
        count[0] += 1
        ins.then_inc(sem, 1)
        engine.wait_ge(sem, count[0])
    return link


def skewed(eng, emit):
    PEEL = 4
    for r in range(PEEL):
        emit(turn(r), turn(r - 1) if r >= 1 else None, turn(r - 2) if r >= 2 else None)
    with eng.Fori(0, (B - PEEL) // 2) as i:
        emit(Turn(2 * i + 4, i + 2, 0), Turn(2 * i + 3, i + 1, 1), Turn(2 * i + 2, i + 1, 0))
        emit(Turn(2 * i + 5, i + 2, 1), Turn(2 * i + 4, i + 2, 0), Turn(2 * i + 3, i + 1, 1))
    emit(None, turn(B - 1), turn(B - 2))
    emit(None, None, turn(B - 1))


def route(nc, k, name, router_dram, E, gate, eps, factor, ctx, rms=None, affine=None):
    EP = max(E, 8)
    sb = lambda n_, shape, dt: k.sb(f"{name}_r_{n_}", shape, dt, ctx)
    sem = lambda n_: k.sem(f"{name}_r_{n_}")
    rt = sb("rt", [P, KD, 2 * E], F32)
    rp = [sb(f"rt{p}", [P, KD, E], BF16) for p in ("hi", "lo")]
    raw = sb("raw", [P, KD, E], F32)
    iota_i, iota = sb("iotai", [T, EP], mybir.dt.int32), sb("iota", [T, EP], F32)
    L = sb("L", [T, B, EP], F32)
    red, m8, idx, idxf = sb("red", [T, B], F32), sb("m8", [T, B, 8], F32), sb("idx", [T, B, 8], U32), sb("idxf", [T, B, 2], F32)
    pick = sb("pick", [T, 2, B, EP], F32)
    ones = sb("ones", [P, T], F32)
    sums = sb("sums", [T, 2 * E], F32)
    r_in, iota_done, parts_done, sums_full, full, exp_ready, exp_done, step = (
        sem(s) for s in ("in", "iota", "parts", "sumsfull", "full", "expready", "exp", "step"))
    over = lambda ap: ap.unsqueeze(2).broadcast_to([T, B, EP])
    logits = k.ps[:T, 0, 0:B * E].rearrange("p (b e) -> p b e", e=E)
    with nc.Block() as block:
        @block.sync
        def _(sp):
            sp.dma_start(raw[:], router_dram).then_inc(r_in, 16)

        @block.gpsimd
        def _(pool):
            nc.gpsimd.iota(iota_i[:], pattern=[[1, EP]], base=0, channel_multiplier=0).then_inc(iota_done, 1)

        @block.tensor
        def _(pe):
            pe.wait_ge(parts_done, 1)
            if affine:
                for t in range(KD):
                    last = nc.tensor.matmul(k.ps[:T, 1, 0:2 * E], ones[:], rt[:, t, :], start=t == 0, stop=t == KD - 1)
                last.then_inc(sums_full, 1)
            for b in range(B):
                last = three_products(nc, logits[:, b, :],
                                      [(k.xT[0][:, t, b * T:(b + 1) * T], k.xT[1][:, t, b * T:(b + 1) * T]) for t in range(KD)],
                                      [(rp[0][:, t, :], rp[1][:, t, :]) for t in range(KD)])
            last.then_inc(full, 1)

        @block.scalar
        def _(act):
            act.wait_ge(exp_ready, 1)
            nc.scalar.activation(L[:], L[:], ACT.Exp).then_inc(exp_done, 1)

        @block.vector
        def _(dve):
            link = linker(dve, step)
            tt, ts = nc.vector.tensor_tensor, nc.vector.tensor_scalar
            dve.wait_ge(r_in, 16)
            dve.wait_ge(iota_done, 1)
            link(nc.vector.tensor_copy(iota[:], iota_i[:]))
            if affine:
                scale, offset, mean, rstd = affine
                link(nc.vector.memset(ones[:], 1.0))
                for t in range(KD):
                    link(ts(rt[:, t, 0:E], raw[:, t, :], scale[:, t:t + 1], None, ALU.mult))
                    link(ts(rt[:, t, E:], raw[:, t, :], offset[:, t:t + 1], None, ALU.mult))
            else:
                link(nc.vector.tensor_copy(rt[:, :, 0:E], raw[:]))
            link(nc.vector.tensor_copy(rp[0][:], rt[:, :, 0:E]))
            tt(rp[1][:], rt[:, :, 0:E], rp[0][:], ALU.subtract).then_inc(parts_done, 1)
            if EP > E:
                link(nc.vector.memset(L[:], -1.0))
            dve.wait_ge(full, 1)
            l = L[:, :, 0:E]
            over_e = lambda ap: ap.unsqueeze(2).broadcast_to([T, B, E])
            if affine:
                dve.wait_ge(sums_full, 1)
                link(nc.vector.tensor_copy(sums[:], k.ps[:T, 1, 0:2 * E]))
                cols = lambda c: sums[:, c:c + E].unsqueeze(1).broadcast_to([T, B, E])
                link(tt(pick[:, 0, :, 0:E], cols(0), over_e(mean), ALU.mult))
                link(tt(l, logits, pick[:, 0, :, 0:E], ALU.subtract))
                link(tt(l, l, over_e(rstd), ALU.mult))
                link(tt(l, l, cols(E), ALU.add))
            else:
                link(tt(l, logits, over_e(rms[:]), ALU.mult))
            link(nc.vector.reduce_max(red[:], l, AX))
            tt(l, l, over_e(red[:]), ALU.subtract).then_inc(exp_ready, 1)
            dve.wait_ge(exp_done, 1)
            link(nc.vector.reduce_sum(red[:], l, AX))
            link(nc.vector.reciprocal(red[:], red[:]))
            link(tt(l, l, over_e(red[:]), ALU.mult))
            if EP > E:
                link(nc.vector.memset(L[:, :, E:], -1.0))
            for b in range(B):
                last = nc.vector.max(m8[:, b, :], L[:, b, :])
            link(last)
            for b in range(B):
                last = nc.vector.max_index(idx[:, b, :], m8[:, b, :], L[:, b, :])
            link(last)
            link(nc.vector.tensor_copy(idxf[:], idx[:, :, 0:2]))
            link(tt(red[:], m8[:, :, 0], m8[:, :, 1], ALU.add))
            link(ts(red[:], red[:], eps, None, ALU.add))
            link(nc.vector.reciprocal(red[:], red[:]))
            link(ts(red[:], red[:], factor, None, ALU.mult))
            for i in range(2):
                link(tt(pick[:, i], iota[:].unsqueeze(1).broadcast_to([T, B, EP]), over(idxf[:, :, i]), ALU.is_equal))
                link(tt(pick[:, i], pick[:, i], over(m8[:, :, i]), ALU.mult))
            link(tt(pick[:, 0], pick[:, 0], pick[:, 1], ALU.add))
            link(tt(gate[:, :, 0:E], pick[:, 0, :, 0:E], over_e(red[:]), ALU.mult))


def l0_experts(nc, k, a):
    with ExitStack() as ctx:
        sb = lambda name, shape, dt: k.sb("f0_" + name, shape, dt, ctx)
        sem = lambda name: k.sem("f0_" + name)
        rms_inv, rms = sb("rmsinv", [T, B], F32), sb("rms", [T, B], F32)
        normalise(nc, k, "n1", rms=(rms_inv, rms))
        gate = sb("gate", [T, B, E0 + E0S], F32)
        with ExitStack() as rctx:
            route(nc, k, "f0", a["F0_router_w"].rearrange("(t p) e -> p t e", p=P), E0, gate, L0_GATE_EPS,
                  k.tg_f[:T, 0:1], rctx, rms=rms)

        raw1 = sb("raw1", [P, 2, KD, HID], F32)
        raw2 = sb("raw2", [P, 2, HM, D], F32)
        w1 = [sb(f"w1{p}", [P, 2, KD, HID], BF16) for p in ("hi", "lo")]
        w2 = [sb(f"w2{p}", [P, 2, HM, D], BF16) for p in ("hi", "lo")]
        rw = sb("rw", [P, E0 + E0S, KD], F32)
        hf = sb("hf", [P, 2, HM, GT], F32)
        hh = sb("hh", [P, 2, HM, GT], BF16)
        hl = sb("hl", [P, 2, HM, GT], BF16)
        w_in = [sem("win0"), sem("win1")]
        rw_in, gate_set, w_hi, w1_lo, w2_lo, up_full, act_done, h_hi, h_lo, y_full, y_used = (
            sem(s) for s in ("rwin", "gateset", "whi", "w1lo", "w2lo", "upfull", "act", "hhi", "hlo", "yfull", "yused"))
        passed = sem("passed")
        UP, DOWN = NG * HM, NG * GB
        FREE_ACT, FREE_HID, FREE_Y, FREE_W1, FREE_W2, DONE_Y = HM, 2 * HM, DOWN, 2 * KD, 2, DOWN

        def experts(eng, emit):
            with eng.Fori(0, E0 // 2) as i:
                emit(2 * i, i, 0, 0, 2 * i)
                emit(2 * i + 1, i, 1, 0, 2 * i + 1)
            for s in range(E0S):
                emit(E0 + s, (E0 + s) // 2, s % 2, 1, s)

        with nc.Block() as block:
            @block.sync
            def _(sp):
                sp.dma_start(rw[:, 0:E0, :], a["F0_rms_w"]).then_inc(rw_in, 16)
                sp.dma_start(rw[:, E0:, :], a["F0_rms_w_s"]).then_inc(rw_in, 16)

                def emit(e, half, odd, shared, i):
                    s1, s2 = ((a["F0_w1"], a["F0_w2"]), (a["F0_w1_s"], a["F0_w2_s"]))[shared]
                    sp.wait_ge(w1_lo, FREE_W1 + KD * (e - 1))
                    sp.sem_inc(passed, 1)
                    sp.wait_ge(w2_lo, FREE_W2 + e - 1)
                    sp.sem_inc(passed, 1)
                    sp.dma_start(raw1[:, odd], s1[bass.ds(i, 1)].rearrange("e (t p) n -> p (e t) n", p=P))\
                        .then_inc(w_in[odd], 16)
                    sp.dma_start(raw2[:, odd], s2[bass.ds(i, 1)].rearrange("e (t p) n -> p (e t) n", p=P))\
                        .then_inc(w_in[odd], 16)
                experts(sp, emit)

            @block.gpsimd
            def _(pool):
                pool.sem_inc(w2_lo, FREE_W2)

                def emit(e, half, odd, shared, i):
                    pool.wait_ge(w_hi, (KD + 1) * (e + 1))
                    nc.gpsimd.tensor_tensor(w2[1][:, odd], raw2[:, odd], w2[0][:, odd], ALU.subtract).then_inc(w2_lo, 1)
                experts(pool, emit)

            @block.tensor
            def _(pe):
                pe.sem_inc(y_full, DONE_Y)

                def emit(e, half, odd, shared, i):
                    pe.wait_ge(w1_lo, FREE_W1 + KD * (e + 1))
                    pe.wait_ge(w2_lo, FREE_W2 + e + 1)
                    for g in range(NG):
                        for m in range(HM):
                            pe.wait_ge(act_done, FREE_ACT + e * UP + g * HM + m + 1 - HM)
                            three_products(nc, k.ps[:, m, :GT],
                                           [(w1[0][:, odd, t, m * P:(m + 1) * P], w1[1][:, odd, t, m * P:(m + 1) * P])
                                            for t in range(KD)],
                                           [(k.xT[0][:, t, g * GT:(g + 1) * GT], k.xT[1][:, t, g * GT:(g + 1) * GT])
                                            for t in range(KD)]).then_inc(up_full, 1)
                        for m in range(HM):
                            pe.wait_ge(h_lo, FREE_HID + e * UP + g * HM + m + 1)
                            for q in range(GB):
                                if m == 0:
                                    pe.wait_ge(y_used, FREE_Y + e * DOWN + g * GB + q + 1 - GB)
                                last = three_products(nc, k.ps[:T, 4 + q, :D],
                                                      [(hh[:, g % 2, m, q * T:(q + 1) * T], hl[:, g % 2, m, q * T:(q + 1) * T])],
                                                      [(w2[0][:, odd, m, :], w2[1][:, odd, m, :])],
                                                      first=m == 0, last=m == HM - 1)
                                if m == HM - 1:
                                    last.then_inc(y_full, 1)
                experts(pe, emit)

            @block.scalar
            def _(act):
                act.sem_inc(act_done, FREE_ACT)

                def emit(e, half, odd, shared, i):
                    for g in range(NG):
                        for m in range(HM):
                            n = g * HM + m
                            act.wait_ge(up_full, e * UP + n + 1)
                            act.wait_ge(h_lo, FREE_HID + e * UP + n + 1 - 2 * HM)
                            nc.scalar.activation(hf[:, g % 2, m, :], k.ps[:, m, :GT], ACT.Silu).then_inc(act_done, 1)
                experts(act, emit)

            @block.vector
            def _(dve):
                dve.sem_inc(h_lo, FREE_HID)
                dve.sem_inc(y_used, FREE_Y)
                dve.sem_inc(w1_lo, FREE_W1)
                for s in range(E0S):
                    for b in range(B):
                        last = nc.vector.tensor_copy(gate[:, b, E0 + s:E0 + s + 1], k.tg_f[:T, 0:1])
                last.then_inc(gate_set, 1)
                dve.wait_ge(gate_set, 1)
                dve.wait_ge(rw_in, 32)

                def split(e, half, odd):
                    dve.wait_ge(w_in[odd], half * 32 + 32)
                    dve.wait_ge(y_full, DONE_Y * e)
                    scale = lambda t: rw[:, bass.ds(e, 1), t]
                    for t in range(KD):
                        nc.vector.tensor_scalar(w1[0][:, odd, t, :], raw1[:, odd, t, :], scale(t), None, ALU.mult).then_inc(w_hi, 1)
                    nc.vector.tensor_copy(w2[0][:, odd], raw2[:, odd]).then_inc(w_hi, 1)
                    for t in range(KD):
                        dve.wait_ge(w_hi, (KD + 1) * e + t + 1)
                        nc.vector.scalar_tensor_tensor(w1[1][:, odd, t, :], raw1[:, odd, t, :], scale(t),
                                                       w1[0][:, odd, t, :], ALU.mult, ALU.subtract).then_inc(w1_lo, 1)
                split(0, 0, 0)

                def emit(e, half, odd, shared, i):
                    for g in range(NG):
                        for m in range(HM):
                            n = g * HM + m
                            dve.wait_ge(act_done, FREE_ACT + e * UP + n + 1)
                            dve.wait_ge(y_full, DONE_Y + e * DOWN + g * GB + GB - 2 * GB)
                            nc.vector.tensor_copy(hh[:, g % 2, m, :], hf[:, g % 2, m, :]).then_inc(h_hi, 1)
                            dve.wait_ge(h_hi, e * UP + n + 1)
                            nc.vector.tensor_tensor(hl[:, g % 2, m, :], hf[:, g % 2, m, :], hh[:, g % 2, m, :],
                                                    ALU.subtract).then_inc(h_lo, 1)
                        for q in range(GB):
                            dve.wait_ge(y_full, DONE_Y + e * DOWN + g * GB + q + 1)
                            dve.wait_ge(y_used, FREE_Y + e * DOWN - DOWN + g * GB + q + 1)
                            nc.vector.scalar_tensor_tensor(k.xs[:, GB * g + q, :], k.ps[:T, 4 + q, :D],
                                                           gate[:, GB * g + q, bass.ds(e, 1)], k.xs[:, GB * g + q, :],
                                                           ALU.mult, ALU.add).then_inc(y_used, 1)
                        if g == 0 and not (isinstance(e, int) and e == E0 + E0S - 1):
                            split(e + 1, half + odd, 1 - odd)
                experts(dve, emit)


def l1_attention(nc, k, a):
    with ExitStack() as ctx:
        sb = lambda name, shape, dt: k.sb("a1_" + name, shape, dt, ctx)
        sem = lambda name: k.sem("a1_" + name)
        normalise(nc, k, "n2")
        wq, wk, wv, wo = load_square(nc, k, "a1", [a["L1_Wq"], a["L1_Wk"], a["L1_Wv"], a["L1_Wo"]],
                                     [None, None, None, k.tg_x[:, 1:2]], ctx)
        bias = sb("bias", [P, 3, KD], F32)
        bk2 = sb("bk2", [P, KD, 2], BF16)
        bo_b = sb("bo", [T, D], F32)
        qT = [sb(f"qT{p}", [P, KD, N], BF16) for p in ("hi", "lo")]
        qkT = [sb(f"qkT{p}", [P, KD, N], BF16) for p in ("hi", "lo")]
        qbk = sb("qbk", [T, B], F32)
        qbk2 = sb("qbk2", [T, B, 2], F32)
        b_in, bo_in, small, full, hi_done, lo_done, bk_full = (
            sem(s) for s in ("bin", "boin", "small", "qfull", "qhi", "qlo", "bkfull"))
        cols = lambda g: slice(g * GT, (g + 1) * GT)

        with nc.Block() as block:
            @block.sync
            def _(sp):
                for i, v in enumerate((a["L1_bq"], a["L1_bk"], a["L1_bv"])):
                    sp.dma_start(bias[:, i, :], v).then_inc(b_in, 16)
                sp.dma_start(bo_b[:], a["L1_bo"].partition_broadcast(T)).then_inc(bo_in, 16)

            @block.tensor
            def _(pe):
                for s, (w, src) in enumerate(((wq, k.xT), (wk, qT))):
                    for g in range(NG):
                        for m in range(KD):
                            n = (s * NG + g) * KD + m
                            if n >= 4:
                                pe.wait_ge(lo_done, n - 3)
                            if s == 1:
                                pe.wait_ge(lo_done, (g + 1) * KD)
                            three_products(nc, k.ps[:, n % 4, :GT],
                                           [(w[0][:, t, m * P:(m + 1) * P], w[1][:, t, m * P:(m + 1) * P]) for t in range(KD)],
                                           [(src[0][:, t, cols(g)], src[1][:, t, cols(g)]) for t in range(KD)]).then_inc(full, 1)
                pe.wait_ge(small, 2)
                for b in range(B):
                    for t in range(KD):
                        for i in range(2):
                            last = nc.tensor.matmul(k.ps[:T, 4, 2 * b:2 * b + 2], qT[i][:, t, b * T:(b + 1) * T],
                                                    bk2[:, t, :], start=t == 0 and i == 0, stop=t == KD - 1 and i == 1)
                last.then_inc(bk_full, 1)

            @block.scalar
            def _(act):
                act.wait_ge(b_in, 48)
                for s, dst in enumerate((qT, qkT)):
                    for g in range(NG):
                        for m in range(KD):
                            n = (s * NG + g) * KD + m
                            act.wait_ge(full, n + 1)
                            nc.scalar.activation(dst[0][:, m, cols(g)], k.ps[:, n % 4, :GT], ACT.Identity,
                                                 bias=bias[:, 0, m:m + 1] if s == 0 else 0.0).then_inc(hi_done, 1)

            @block.vector
            def _(dve):
                dve.wait_ge(b_in, 48)
                nc.vector.tensor_copy(bk2[:, :, 0], bias[:, 1, :]).then_inc(small, 1)
                dve.wait_ge(small, 1)
                nc.vector.tensor_tensor(bk2[:, :, 1], bias[:, 1, :], bk2[:, :, 0], ALU.subtract).then_inc(small, 1)
                dve.wait_ge(bo_in, 16)
                nc.vector.tensor_scalar(bo_b[:], bo_b[:], k.tg_x[:T, 1:2], None, ALU.mult).then_inc(small, 1)
                for s, dst in enumerate((qT, qkT)):
                    for g in range(NG):
                        for m in range(KD):
                            n = (s * NG + g) * KD + m
                            dve.wait_ge(hi_done, n + 1)
                            if s == 0:
                                last = nc.vector.scalar_tensor_tensor(dst[1][:, m, cols(g)], k.ps[:, n % 4, :GT],
                                                                      bias[:, 0, m:m + 1], dst[0][:, m, cols(g)],
                                                                      ALU.add, ALU.subtract)
                            else:
                                last = nc.vector.tensor_tensor(dst[1][:, m, cols(g)], k.ps[:, n % 4, :GT],
                                                               dst[0][:, m, cols(g)], ALU.subtract)
                            last.then_inc(lo_done, 1)
                dve.wait_ge(bk_full, 1)
                nc.vector.tensor_copy(qbk2[:], k.ps[:T, 4, 0:2 * B].rearrange("p (b two) -> p b two", two=2)).then_inc(small, 1)
                dve.wait_ge(small, 4)
                nc.vector.tensor_tensor(qbk[:], qbk2[:, :, 0], qbk2[:, :, 1], ALU.add).then_inc(small, 1)
                dve.wait_ge(small, 5)
                dve.wait_ge(lo_done, 2 * NG * KD)

        cT = sb("cT", [P, 2, KD, S], F32)
        cTp = [sb(f"cT{p}", [P, 2, KD, S], BF16) for p in ("hi", "lo")]
        cR = sb("cR", [C, 2, SC, D], F32)
        cRp = [sb(f"cR{p}", [C, 2, SC, D], BF16) for p in ("hi", "lo")]
        pr = sb("pr", [T, 2, S], F32)
        pT = [sb(f"pT{p}", [C, 2, SC, T], BF16) for p in ("hi", "lo")]
        mT = [sb(f"mT{p}", [P, KD, N], BF16) for p in ("hi", "lo")]
        scale_t = sb("scale", [T, 1], F32)
        small_t = sb("small", [T, 2, 4], F32)
        c_in = [sem("cin0"), sem("cin1")]
        (ct_hi, ct_lo, cr_hi, cr_lo, s_full, bias_step, p_done, pn_done, t_full, pt_hi, pt_lo, m_full, m_hi, m_lo) = (
            sem(s) for s in ("cthi", "ctlo", "crhi", "crlo", "sfull", "biasstep", "pdone", "pndone", "tfull", "pthi",
                             "ptlo", "mfull", "mhi", "mlo"))
        SCALE = D ** -0.5
        pn_done_r, scale_set, passed = sem("rsum"), sem("scaleset"), sem("passed")
        row = lambda b: bass.ds(b.b * T, T)
        one = lambda ap, b: ap[:, bass.ds(b.b, 1)]

        with nc.Block() as block:
            @block.sync
            def _(sp):
                with sp.Fori(0, B // 2) as i:
                    for o in range(2):
                        b = 2 * i + o
                        sp.wait_ge(ct_lo, b + 1)
                        sp.sem_inc(passed, 1)
                        sp.dma_start(cT[:, o], a["ctxT"][bass.ds(b, 1)].rearrange("b (t p) s -> p (b t) s", p=P)).then_inc(c_in[o], 16)
                        sp.wait_ge(cr_lo, b + 1)
                        sp.sem_inc(passed, 1)
                        sp.dma_start(cR[:, o], a["ctx"][bass.ds(b, 1)].rearrange("b (c p) d -> p (b c) d", p=C)).then_inc(c_in[o], 16)

            @block.gpsimd
            def _(pool):
                pool.sem_inc(cr_lo, 2)

                def emit(s, t, m):
                    if s is None:
                        return
                    pool.wait_ge(cr_hi, s.b + 1)
                    pool.wait_ge(m_full, 3 + s.b - 1)
                    nc.gpsimd.tensor_tensor(cRp[1][:, s.odd], cR[:, s.odd], cRp[0][:, s.odd],
                                            ALU.subtract).then_inc(cr_lo, 1)
                skewed(pool, emit)

            @block.tensor
            def _(pe):
                pe.sem_inc(m_full, 3)

                def emit(s, t, m):
                    if s is not None:
                        pe.wait_ge(ct_lo, s.b + 3)
                        at_least(pe, p_done, s.b - 1)
                        three_products(nc, k.ps[:T, s.odd, :S],
                                       [(qkT[0][:, i, row(s)], qkT[1][:, i, row(s)]) for i in range(KD)],
                                       [(cTp[0][:, s.odd, i, :], cTp[1][:, s.odd, i, :]) for i in range(KD)]).then_inc(s_full, 1)
                    if t is not None:
                        pe.wait_ge(pn_done, t.b + 1)
                        at_least(pe, pt_lo, t.b - 1)
                        for c in range(SC):
                            last = nc.tensor.transpose(k.ps[:C, 2 + t.odd, c * T:(c + 1) * T],
                                                       pr[:, t.odd, c * C:(c + 1) * C], k.ident[:T, :T])
                        last.then_inc(t_full, 1)
                    if m is not None:
                        pe.wait_ge(pt_lo, m.b + 1)
                        pe.wait_ge(cr_lo, m.b + 3)
                        pe.wait_ge(m_lo, m.b)
                        for i in range(KD):
                            last = three_products(nc, k.ps[:, 4 + m.odd, i * T:(i + 1) * T],
                                                  [(cRp[0][:, m.odd, c, i * P:(i + 1) * P], cRp[1][:, m.odd, c, i * P:(i + 1) * P])
                                                   for c in range(SC)],
                                                  [(pT[0][:, m.odd, c, :], pT[1][:, m.odd, c, :]) for c in range(SC)])
                        last.then_inc(m_full, 1)
                skewed(pe, emit)

            @block.scalar
            def _(act):
                def emit(s, t, m):
                    if s is not None:
                        act.wait_ge(c_in[s.odd], s.half * 32 + 32)
                        at_least(act, s_full, s.b - 1)
                        nc.scalar.activation(cTp[0][:, s.odd], cT[:, s.odd], ACT.Copy).then_inc(ct_hi, 1)
                        act.wait_ge(m_full, 3 + s.b - 1)
                        nc.scalar.activation(cRp[0][:, s.odd], cR[:, s.odd], ACT.Copy).then_inc(cr_hi, 1)
                        act.wait_ge(bias_step, 3 * s.b + 3)
                        at_least(act, t_full, s.b - 1)
                        nc.scalar.activation(pr[:, s.odd, :], k.ps[:T, s.odd, :S], ACT.Exp, bias=small_t[:, s.odd, 1:2],
                                             scale=SCALE, accum_out=small_t[:, s.odd, 2:3]).then_inc(p_done, 1)
                    if t is not None:
                        act.wait_ge(t_full, t.b + 1)
                        act.wait_ge(m_full, 3 + t.b - 1)
                        nc.scalar.activation(pT[0][:, t.odd], k.ps[:C, 2 + t.odd, 0:SC * T].rearrange("p (c q) -> p c q", c=SC),
                                             ACT.Copy).then_inc(pt_hi, 1)
                    if m is not None:
                        act.wait_ge(m_full, 3 + m.b + 1)
                        nc.scalar.activation(mT[0][:, :, row(m)], k.ps[:, 4 + m.odd, 0:KD * T].rearrange("p (c q) -> p c q", c=KD),
                                             ACT.Copy).then_inc(m_hi, 1)
                skewed(act, emit)

            @block.vector
            def _(dve):
                dve.sem_inc(ct_lo, 2)
                dve.sem_inc(m_lo, 1)

                def emit(s, t, m):
                    if s is not None:
                        dve.wait_ge(ct_hi, s.b + 1)
                        nc.vector.tensor_tensor(cTp[1][:, s.odd], cT[:, s.odd], cTp[0][:, s.odd], ALU.subtract).then_inc(ct_lo, 1)
                    if t is not None:
                        dve.wait_ge(p_done, t.b + 1)
                        nc.vector.reciprocal(small_t[:, t.odd, 3:4], small_t[:, t.odd, 2:3]).then_inc(pn_done_r, 1)
                        dve.wait_ge(pn_done_r, t.b + 1)
                        nc.vector.tensor_scalar(pr[:, t.odd, :], pr[:, t.odd, :], small_t[:, t.odd, 3:4], None,
                                                ALU.mult).then_inc(pn_done, 1)
                    if s is not None:
                        dve.wait_ge(s_full, s.b + 1)
                        at_least(dve, p_done, s.b - 1)
                        nc.vector.reduce_max(small_t[:, s.odd, 0:1], k.ps[:T, s.odd, :S], AX).then_inc(bias_step, 1)
                        dve.wait_ge(bias_step, 3 * s.b + 1)
                        nc.vector.tensor_tensor(small_t[:, s.odd, 0:1], small_t[:, s.odd, 0:1], one(qbk, s), ALU.add).then_inc(bias_step, 1)
                        dve.wait_ge(bias_step, 3 * s.b + 2)
                        nc.vector.scalar_tensor_tensor(small_t[:, s.odd, 1:2], one(qbk, s), small_t[:, s.odd, 0:1],
                                                       scale_t[:], ALU.subtract, ALU.mult).then_inc(bias_step, 1)
                    if t is not None:
                        dve.wait_ge(pt_hi, t.b + 1)
                        nc.vector.tensor_tensor(pT[1][:, t.odd], k.ps[:C, 2 + t.odd, 0:SC * T].rearrange("p (c q) -> p c q", c=SC),
                                                pT[0][:, t.odd], ALU.subtract).then_inc(pt_lo, 1)
                    if m is not None:
                        dve.wait_ge(m_hi, m.b + 1)
                        nc.vector.tensor_tensor(mT[1][:, :, row(m)], k.ps[:, 4 + m.odd, 0:KD * T].rearrange("p (c q) -> p c q", c=KD),
                                                mT[0][:, :, row(m)], ALU.subtract).then_inc(m_lo, 1)
                nc.vector.memset(scale_t[:], SCALE).then_inc(scale_set, 1)
                dve.wait_ge(scale_set, 1)
                skewed(dve, emit)

        tmp = sb("tmp", [P, 2, GT], F32)
        uT = [sb(f"uT{p}", [P, 2, KD, GT], BF16) for p in ("hi", "lo")]
        v_full, v_used, u_step, u_hi, u_lo, y_full, y_used, sum_done = (
            sem(s) for s in ("vfull", "vused", "ustep", "uhi", "ulo", "yfull", "yused", "sumdone"))
        with nc.Block() as block:
            @block.tensor
            def _(pe):
                def values(g):
                    for m in range(KD):
                        n = g * KD + m
                        if n >= 2:
                            pe.wait_ge(v_used, n - 1)
                        three_products(nc, k.ps[:, n % 2, :GT],
                                       [(wv[0][:, t, m * P:(m + 1) * P], wv[1][:, t, m * P:(m + 1) * P]) for t in range(KD)],
                                       [(mT[0][:, t, cols(g)], mT[1][:, t, cols(g)]) for t in range(KD)]).then_inc(v_full, 1)
                values(0)
                for g in range(NG):
                    if g + 1 < NG:
                        values(g + 1)
                    pe.wait_ge(u_lo, KD * (g + 1))
                    for i in range(GB):
                        n = GB * g + i
                        if n >= 4:
                            pe.wait_ge(y_used, n - 3)
                        three_products(nc, k.ps[:T, 4 + n % 4, :D],
                                       [(uT[0][:, g % 2, t, i * T:(i + 1) * T], uT[1][:, g % 2, t, i * T:(i + 1) * T])
                                        for t in range(KD)],
                                       [(wo[0][:, t, :], wo[1][:, t, :]) for t in range(KD)]).then_inc(y_full, 1)

            @block.vector
            def _(dve):
                def u(g):
                    for m in range(KD):
                        n = g * KD + m
                        dve.wait_ge(v_full, n + 1)
                        if n >= 2:
                            dve.wait_ge(u_lo, n - 1)
                        nc.vector.scalar_tensor_tensor(tmp[:, n % 2, :], k.ps[:, n % 2, :GT], bias[:, 2, m:m + 1],
                                                       k.xT[0][:, m, cols(g)], ALU.add, ALU.add).then_inc(v_used, 1)
                        dve.wait_ge(v_used, n + 1)
                        nc.vector.tensor_tensor(tmp[:, n % 2, :], tmp[:, n % 2, :], k.xT[1][:, m, cols(g)], ALU.add).then_inc(u_step, 1)
                        dve.wait_ge(u_step, n + 1)
                        if g >= 2:
                            dve.wait_ge(y_full, GB * (g - 1))
                        nc.vector.tensor_copy(uT[0][:, g % 2, m, :], tmp[:, n % 2, :]).then_inc(u_hi, 1)
                        dve.wait_ge(u_hi, n + 1)
                        nc.vector.tensor_tensor(uT[1][:, g % 2, m, :], tmp[:, n % 2, :], uT[0][:, g % 2, m, :],
                                                ALU.subtract).then_inc(u_lo, 1)
                u(0)
                for g in range(NG):
                    if g + 1 < NG:
                        u(g + 1)
                    for i in range(GB):
                        n = GB * g + i
                        dve.wait_ge(y_full, n + 1)
                        nc.vector.tensor_tensor(k.xs[:, n, :], k.ps[:T, 4 + n % 4, :D], k.xs[:, n, :], ALU.add).then_inc(y_used, 1)
                        dve.wait_ge(y_used, n + 1)
                        nc.vector.tensor_tensor(k.xs[:, n, :], k.xs[:, n, :], bo_b[:], ALU.add).then_inc(sum_done, 1)
                dve.wait_ge(sum_done, B)


def l1_experts(nc, k, a):
    with ExitStack() as ctx:
        sb = lambda name, shape, dt: k.sb("f1_" + name, shape, dt, ctx)
        sem = lambda name: k.sem("f1_" + name)
        mv2, rstd2 = sb("mv2", [T, B, 2], F32), sb("rstd2", [T, B], F32)
        normalise(nc, k, "n3", again=(mv2, rstd2))
        gate = sb("gate", [T, B, E1], F32)
        rn = sb("rn", [P, 2, KD], F32)
        ln = sb("ln", [P, 2, E1, HM], F32)
        on = sb("on", [T, 2, D], F32)
        raw1 = sb("raw1", [P, 2, KD, HID], F32)
        raw2 = sb("raw2", [P, 2, HM, D], F32)
        w1 = [sb(f"w1{p}", [P, E1, KD, HID], BF16) for p in ("hi", "lo")]
        w2 = [sb(f"w2{p}", [P, E1, HM, D], BF16) for p in ("hi", "lo")]
        w_in = [sem("win0"), sem("win1")]
        rn_in, vec_in, on_done, w1_hi, w1_lo, w2_hi, w2_lo = (
            sem(s) for s in ("rnin", "vecin", "on", "w1hi", "w1lo", "w2hi", "w2lo"))
        with nc.Block() as block:
            @block.sync
            def _(sp):
                for i, n in enumerate(("rn_g", "rn_b")):
                    sp.dma_start(rn[:, i, :], a["F1_" + n]).then_inc(rn_in, 16)
                for i, n in enumerate(("ln_g", "ln_b")):
                    sp.dma_start(ln[:, i], a["F1_" + n]).then_inc(vec_in, 16)
                for i, n in enumerate(("on_g", "on_b")):
                    sp.dma_start(on[:, i, :], a["F1_" + n].partition_broadcast(T)).then_inc(vec_in, 16)
                for e in range(E1):
                    if e >= 2:
                        sp.wait_ge(w1_lo, e - 1)
                        sp.wait_ge(w2_lo, e - 1)
                    sp.dma_start(raw1[:, e % 2], a["F1_w1"][e].rearrange("(t p) n -> p t n", p=P)).then_inc(w_in[e % 2], 16)
                    sp.dma_start(raw2[:, e % 2], a["F1_w2"][e].rearrange("(t p) n -> p t n", p=P)).then_inc(w_in[e % 2], 16)

            @block.scalar
            def _(act):
                for e in range(E1):
                    act.wait_ge(w_in[e % 2], 32 * (e // 2 + 1))
                    nc.scalar.activation(w1[0][:, e], raw1[:, e % 2], ACT.Copy).then_inc(w1_hi, 1)
                    nc.scalar.activation(w2[0][:, e], raw2[:, e % 2], ACT.Copy).then_inc(w2_hi, 1)

            @block.vector
            def _(dve):
                for e in range(E1):
                    dve.wait_ge(w1_hi, e + 1)
                    nc.vector.tensor_tensor(w1[1][:, e], raw1[:, e % 2], w1[0][:, e], ALU.subtract).then_inc(w1_lo, 1)
                    dve.wait_ge(w2_hi, e + 1)
                    nc.vector.tensor_tensor(w2[1][:, e], raw2[:, e % 2], w2[0][:, e], ALU.subtract).then_inc(w2_lo, 1)
                dve.wait_ge(vec_in, 64)
                nc.vector.tensor_scalar(on[:], on[:], k.tg_f[:T, 1:2], None, ALU.mult).then_inc(on_done, 1)
                dve.wait_ge(on_done, 1)
                dve.wait_ge(w2_lo, E1)
                dve.wait_ge(rn_in, 32)

        with ExitStack() as rctx:
            route(nc, k, "f1", a["F1_router_w"].rearrange("(t p) e -> p t e", p=P), E1, gate, L1_GATE_EPS,
                  1.0, rctx, affine=(rn[:, 0, :], rn[:, 1, :], mv2[:, :, 0], rstd2[:]))

        acc = sb("acc", [T, B, D], F32)
        stats, mv = sb("stats", [T, 2, 6], F32), sb("mv", [T, 2, 2], F32)
        std, rstd, shift, eps = (sb(n, [T, 2], F32) for n in ("std", "rstd", "shift", "eps"))
        z = sb("z", [T, 2, HID], F32)
        rf = sb("rf", [P, 2, HM, T], F32)
        rh, rl = sb("rh", [P, 2, HM, T], BF16), sb("rl", [P, 2, HM, T], BF16)
        (eps_set, up_full, st_done, var_done, std_done, rstd_done, shift_done, z_done, t_full, relu_done, r_hi, r_lo,
         y_full, y_used) = (sem(s) for s in ("epsset", "upfull", "st", "var", "std", "rstd", "shift", "z", "tfull",
                                             "relu", "rhi", "rlo", "yfull", "yused"))

        passed = sem("passed")

        class Unit:
            def __init__(self, e, r):
                self.e, self.r, self.b, self.odd, self.n = e, r, r.b, r.odd, e * B + r.b

        def units(eng, emit):
            for e in range(E1):
                PEEL = 2 if e else 4
                before = lambda r: Unit(e, turn(r)) if r >= 0 else Unit(e - 1, turn(B + r)) if e else None
                for r in range(PEEL):
                    emit(Unit(e, turn(r)), before(r - 1), before(r - 2))
                h = PEEL // 2
                with eng.Fori(0, (B - PEEL) // 2) as i:
                    at = lambda r: Unit(e, Turn(2 * (i + h) + r, i + h + r // 2, r % 2))
                    emit(at(0), at(-1), at(-2))
                    emit(at(1), at(0), at(-1))
            emit(None, Unit(E1 - 1, turn(B - 1)), Unit(E1 - 1, turn(B - 2)))
            emit(None, None, Unit(E1 - 1, turn(B - 1)))

        with nc.Block() as block:
            @block.tensor
            def _(pe):
                def emit(s, t, m):
                    if s is not None:
                        at_least(pe, z_done, s.n - 1)
                        three_products(nc, k.ps[:T, s.odd, :],
                                       [(k.xT[0][:, i, bass.ds(s.b * T, T)], k.xT[1][:, i, bass.ds(s.b * T, T)]) for i in range(KD)],
                                       [(w1[0][:, s.e, i, :], w1[1][:, s.e, i, :]) for i in range(KD)]).then_inc(up_full, 1)
                    if t is not None:
                        pe.wait_ge(z_done, t.n + 1)
                        at_least(pe, relu_done, HM * (t.n - 1))
                        for i in range(HM):
                            last = nc.tensor.transpose(k.ps[:, 2 + t.odd, i * T:(i + 1) * T], z[:, t.odd, i * P:(i + 1) * P],
                                                       k.ident[:T, :T])
                        last.then_inc(t_full, 1)
                    if m is not None:
                        pe.wait_ge(r_lo, m.n + 1)
                        pe.wait_ge(y_used, m.n)
                        three_products(nc, k.ps[:T, 4 + m.odd, :D],
                                       [(rh[:, m.odd, i, :], rl[:, m.odd, i, :]) for i in range(HM)],
                                       [(w2[0][:, m.e, i, :], w2[1][:, m.e, i, :]) for i in range(HM)]).then_inc(y_full, 1)
                units(pe, emit)

            @block.scalar
            def _(act):
                act.wait_ge(eps_set, 1)

                def emit(s, t, m):
                    if s is not None:
                        act.wait_ge(var_done, s.n + 1)
                        at_least(act, rstd_done, s.n - 1)
                        nc.scalar.activation(std[:, s.odd:s.odd + 1], mv[:, s.odd, 1:2], ACT.Sqrt, bias=eps[:, 0:1]).then_inc(std_done, 1)
                    if t is not None:
                        act.wait_ge(t_full, t.n + 1)
                        at_least(act, r_lo, t.n - 1)
                        for i in range(HM):
                            nc.scalar.activation(rf[:, t.odd, i, :], k.ps[:, 2 + t.odd, i * T:(i + 1) * T], ACT.Relu,
                                                 bias=ln[:, 1, t.e, i:i + 1], scale=ln[:, 0, t.e, i:i + 1]).then_inc(relu_done, 1)
                    if s is not None:
                        act.wait_ge(shift_done, s.n + 1)
                        at_least(act, t_full, s.n - 1)
                        nc.scalar.activation(z[:, s.odd, :], k.ps[:T, s.odd, :], ACT.Identity, bias=shift[:, s.odd:s.odd + 1],
                                             scale=rstd[:, s.odd:s.odd + 1]).then_inc(z_done, 1)
                units(act, emit)

            @block.gpsimd
            def _(pool):
                def emit(s, t, m):
                    if t is not None:
                        pool.wait_ge(r_hi, t.n + 1)
                        at_least(pool, y_full, t.n - 1)
                        nc.gpsimd.tensor_tensor(rl[:, t.odd], rf[:, t.odd], rh[:, t.odd], ALU.subtract).then_inc(r_lo, 1)
                units(pool, emit)

            @block.vector
            def _(dve):
                dve.sem_inc(y_used, 1)
                nc.vector.memset(eps[:], LN_EPS).then_inc(eps_set, 1)
                dve.wait_ge(eps_set, 1)

                def emit(s, t, m):
                    if s is not None:
                        dve.wait_ge(up_full, s.n + 1)
                        nc.vector.bn_stats(stats[:, s.odd, :], k.ps[:T, s.odd, :]).then_inc(st_done, 1)
                        at_least(dve, std_done, s.n - 1)
                        dve.wait_ge(st_done, s.n + 1)
                        dve.sem_inc(passed, 1)
                        nc.vector.bn_aggr(mv[:, s.odd, :], stats[:, s.odd, :]).then_inc(var_done, 1)
                        dve.wait_ge(std_done, s.n + 1)
                        at_least(dve, z_done, s.n - 1)
                        nc.vector.reciprocal(rstd[:, s.odd:s.odd + 1], std[:, s.odd:s.odd + 1]).then_inc(rstd_done, 1)
                        dve.wait_ge(rstd_done, s.n + 1)
                        nc.vector.scalar_tensor_tensor(shift[:, s.odd:s.odd + 1], mv[:, s.odd, 0:1], -1.0, rstd[:, s.odd:s.odd + 1],
                                                       ALU.mult, ALU.mult).then_inc(shift_done, 1)
                    if t is not None:
                        dve.wait_ge(relu_done, HM * t.n + HM)
                        at_least(dve, y_full, t.n - 1)
                        nc.vector.tensor_copy(rh[:, t.odd], rf[:, t.odd]).then_inc(r_hi, 1)
                    if m is not None:
                        dve.wait_ge(y_full, m.n + 1)
                        y, o, g = k.ps[:T, 4 + m.odd, :D], acc[:, bass.ds(m.b, 1), :].rearrange("p o d -> p (o d)"), gate[:, bass.ds(m.b, 1), m.e]
                        if m.e == 0:
                            nc.vector.tensor_scalar(o, y, g, None, ALU.mult).then_inc(y_used, 1)
                        else:
                            dve.wait_ge(y_used, m.n - B + 2)
                            nc.vector.scalar_tensor_tensor(o, y, g, o, ALU.mult, ALU.add).then_inc(y_used, 1)
                units(dve, emit)

        s_all, stats_all = sb("sall", [T, B], F32), sb("statsall", [T, B, 6], F32)
        a_done, v_done, sq_done, r_done, n_done, g_done, add_done, x_done, stored = (
            sem(s) for s in ("ostat", "ovar", "osq", "or", "on1", "on2", "on3", "ox", "stored"))
        with nc.Block() as block:
            @block.vector
            def _(dve):
                for b in range(B):
                    nc.vector.bn_stats(stats_all[:, b, :], acc[:, b, :]).then_inc(a_done, 1)
                for b in range(B):
                    dve.wait_ge(a_done, b + 1)
                    nc.vector.bn_aggr(k.mv[:, b, :], stats_all[:, b, :]).then_inc(v_done, 1)
                dve.wait_ge(sq_done, 1)
                nc.vector.reciprocal(k.rstd[:], s_all[:]).then_inc(r_done, 1)
                dve.wait_ge(r_done, 1)
                for b in range(B):
                    nc.vector.tensor_scalar(acc[:, b, :], acc[:, b, :], k.mv[:, b, 0:1], k.rstd[:, b:b + 1],
                                            ALU.subtract, ALU.mult).then_inc(n_done, 1)
                for g in range(NG):
                    r = slice(GB * g, GB * (g + 1))
                    wide = lambda i: on[:, i, :].unsqueeze(1).broadcast_to([T, GB, D])
                    dve.wait_ge(n_done, GB * (g + 1))
                    nc.vector.tensor_tensor(acc[:, r, :], acc[:, r, :], wide(0), ALU.mult).then_inc(g_done, 1)
                    nc.vector.tensor_tensor(k.xs[:, r, :], k.xs[:, r, :], wide(1), ALU.add).then_inc(add_done, 1)
                    dve.wait_ge(g_done, g + 1)
                    dve.wait_ge(add_done, g + 1)
                    nc.vector.tensor_tensor(k.xs[:, r, :], k.xs[:, r, :], acc[:, r, :], ALU.add).then_inc(x_done, 1)

            @block.scalar
            def _(act):
                act.wait_ge(v_done, B)
                nc.scalar.activation(s_all[:], k.mv[:, :, 1], ACT.Sqrt, bias=eps[:, 0:1]).then_inc(sq_done, 1)

            @block.sync
            def _(sp):
                for g in range(NG):
                    sp.wait_ge(x_done, g + 1)
                    sp.dma_start(a["out"][GB * g:GB * (g + 1)].rearrange("b t d -> t b d"),
                                 k.xs[:, GB * g:GB * (g + 1), :]).then_inc(stored, 16)
                sp.wait_ge(stored, 16 * NG)


def store(nc, k, out):
    stored = k.sem("stored")
    with nc.Block() as block:
        @block.sync
        def _(sp):
            sp.dma_start(out.rearrange("b t d -> t b d"), k.xs[:]).then_inc(stored, 16)
            sp.wait_ge(stored, 16)


def build(nc, a, out, stages=4):
    a = dict(a, out=out)
    with ExitStack() as ctx:
        k = Core(nc, ctx)
        setup(nc, k, a["x"], a["g_xattn"], a["g_ffn"])
        normalise(nc, k, "n0")
        l0_attention(nc, k, a["ctxT"], a["L0_Wq"], a["L0_bq"], a["L0_Wk"], a["L0_bk"], a["L0_Wv"], a["L0_bv"],
                     a["L0_Wo"], a["L0_bo"])
        k.release()
        if stages >= 2:
            l0_experts(nc, k, a)
            k.release()
        if stages >= 3:
            l1_attention(nc, k, a)
            k.release()
        if stages >= 4:
            l1_experts(nc, k, a)
        else:
            store(nc, k, out)


def kernel(**inputs):
    import numpy as np
    import concourse.bacc as bacc
    from concourse import mybir as m
    from concourse.bass_utils import run_bass_kernel_spmd

    keep = np.ascontiguousarray
    by_feature = lambda v: keep(np.reshape(v, (KD, P)).T)
    of = {n: np.asarray(v) for n, v in inputs.items()}
    a = {"x": of["x"], "ctx": of["ctx_1024"], "ctxT": np.transpose(of["ctx_1024"], (0, 2, 1)),
         "g_xattn": of["g_xattn"], "g_ffn": of["g_ffn"], "L1_Wk": of["L1_xattn_Wk"]}
    for n in ("Wq", "Wk", "Wv"):
        a["L0_" + n] = np.reshape(np.transpose(of["L0_xattn_" + n], (1, 0, 2)), (D, D))
    a["L0_Wo"] = of["L0_xattn_Wo"]
    for n in ("Wq", "Wv", "Wo"):
        a["L1_" + n] = of["L1_xattn_" + n].T
    for layer in ("L0", "L1"):
        for n in ("bq", "bk", "bv"):
            a[f"{layer}_{n}"] = by_feature(of[f"{layer}_xattn_{n}"])
        a[f"{layer}_bo"] = of[f"{layer}_xattn_bo"]
    for n in ("router_w", "w1", "w2", "w1_s", "w2_s"):
        a["F0_" + n] = of["L0_ffn_" + n]
    for n in ("rms_w", "rms_w_s"):
        v = of["L0_ffn_" + n]
        a["F0_" + n] = np.transpose(np.reshape(v, (v.shape[0], KD, P)), (2, 0, 1))
    for n in ("w1", "w2", "on_g", "on_b"):
        a["F1_" + n] = of["L1_ffn_" + n]
    a["F1_router_w"] = of["L1_ffn_router_w"].T
    for n in ("rn_g", "rn_b"):
        a["F1_" + n] = by_feature(of["L1_ffn_" + n])
    for n in ("ln_g", "ln_b"):
        a["F1_" + n] = np.transpose(np.reshape(of["L1_ffn_" + n], (E1, HM, P)), (2, 0, 1))
    a = {n: keep(v) for n, v in a.items()}

    nc = bacc.Bacc("TRN2", target_bir_lowering=False, num_devices=1)
    args = {n: nc.dram_tensor(n, v.shape, m.dt.from_np(v.dtype), kind="ExternalInput").ap() for n, v in a.items()}
    out = nc.dram_tensor("out", (B, T, D), m.dt.float32, kind="ExternalOutput").ap()
    build(nc, args, out)
    return run_bass_kernel_spmd(nc, [a], core_ids=[0]).results[0]["out"]
```
